# Optimizing a Trainium2 kernel written in Bass

```python
import numpy as np
import jax
import jax.numpy as jnp

def _softmax(x, axis=-1):
    return jax.nn.softmax(x, axis=axis)

def _gelu(x):
    return jax.nn.gelu(x, approximate=True)

def _silu(x):
    return jax.nn.silu(x)

def _sigmoid(x):
    return jax.nn.sigmoid(x)

def _layernorm(x, axis=-1, eps=1e-05):
    m = jnp.mean(x, axis=axis, keepdims=True)
    v = jnp.var(x, axis=axis, keepdims=True)
    return (x - m) / jnp.sqrt(v + eps)

def _scatter_add(tgt, idx, src, axis=0):
    return tgt.at[idx].add(src)

def _segment_sum(src, seg, n):
    return jax.ops.segment_sum(src, seg, n)
kernel_name = 'mk_macaron_d1_jaxref_r8_ddedc5'

def setup_inputs(seed: int=0):
    np.random.seed(seed)
    _w = jnp.asarray

    def _L0_attn_setup():
        import jax, jax.numpy as jnp
        import numpy as np
        B, T, D = (1, 256, 128)
        H = 16
        SEM_DIM, GEO_DIM, ATTN_DIM = (64, 64, 128)
        ROPE_BASE = 10000.0
        NEG = -1000000000.0

        def _heads(y, hd):
            b, t, _ = y.shape
            return y.reshape(b, t, H, hd).transpose(0, 2, 1, 3)

        def _rope(x, cos, sin):
            hd = x.shape[-1]
            x1, x2 = (x[..., :hd // 2], x[..., hd // 2:])
            c = cos[None, None]
            sn = sin[None, None]
            return jnp.concatenate([x1 * c - x2 * sn, x2 * c + x1 * sn], axis=-1)

        def _forward(x, wq_sem, wk_sem, wq_geo, wk_geo, wv, wo, k_sem_null, k_geo_null, v_null):
            b, t, _ = x.shape
            sem_hd = wq_sem.shape[1] // H
            geo_hd = wq_geo.shape[1] // H
            v_hd = wv.shape[1] // H
            sem_scale = 1.0 / np.sqrt(sem_hd)
            geo_scale = 1.0 / np.sqrt(geo_hd)
            qs = _heads(x @ wq_sem, sem_hd)
            ks = _heads(x @ wk_sem, sem_hd)
            qg = _heads(x @ wq_geo, geo_hd)
            kg = _heads(x @ wk_geo, geo_hd)
            v = _heads(x @ wv, v_hd)
            pos = jnp.arange(t, dtype=jnp.float32)
            inv_freq = 1.0 / ROPE_BASE ** (jnp.arange(0, geo_hd, 2, dtype=jnp.float32) / geo_hd)
            ang = pos[:, None] * inv_freq[None, :]
            cos, sin = (jnp.cos(ang), jnp.sin(ang))
            qg = _rope(qg, cos, sin)
            kg = _rope(kg, cos, sin)
            ksn = jnp.broadcast_to(k_sem_null.reshape(1, 1, H, sem_hd).transpose(0, 2, 1, 3), (b, H, 1, sem_hd))
            kgn = jnp.broadcast_to(k_geo_null.reshape(1, 1, H, geo_hd).transpose(0, 2, 1, 3), (b, H, 1, geo_hd))
            vn = jnp.broadcast_to(v_null.reshape(1, 1, H, v_hd).transpose(0, 2, 1, 3), (b, H, 1, v_hd))
            ks_full = jnp.concatenate([ksn, ks], axis=2)
            kg_full = jnp.concatenate([kgn, kg], axis=2)
            v_full = jnp.concatenate([vn, v], axis=2)
            scores = jnp.einsum('bhqd,bhkd->bhqk', qs, ks_full).astype(jnp.float32) * sem_scale + jnp.einsum('bhqd,bhkd->bhqk', qg, kg_full).astype(jnp.float32) * geo_scale
            causal = jnp.tril(jnp.ones((t, t), dtype=bool))
            mask = jnp.concatenate([jnp.ones((t, 1), dtype=bool), causal], axis=1)
            scores = jnp.where(mask[None, None], scores, NEG)
            probs = jax.nn.softmax(scores, axis=-1).astype(v.dtype)
            out = jnp.einsum('bhqk,bhkd->bhqd', probs, v_full)
            out = out.transpose(0, 2, 1, 3).reshape(b, t, H * v_hd)
            return out @ wo
        key = jax.random.key(seed)
        ks = jax.random.split(key, 10)
        s = 0.02
        return {'x': jax.random.normal(ks[0], (B, T, D), jnp.float32), 'wq_sem': jax.random.normal(ks[1], (D, SEM_DIM), jnp.float32) * s, 'wk_sem': jax.random.normal(ks[2], (D, SEM_DIM), jnp.float32) * s, 'wq_geo': jax.random.normal(ks[3], (D, GEO_DIM), jnp.float32) * s, 'wk_geo': jax.random.normal(ks[4], (D, GEO_DIM), jnp.float32) * s, 'wv': jax.random.normal(ks[5], (D, ATTN_DIM), jnp.float32) * s, 'wo': jax.random.normal(ks[6], (ATTN_DIM, D), jnp.float32) * s, 'k_sem_null': jax.random.normal(ks[7], (SEM_DIM,), jnp.float32) * s, 'k_geo_null': jax.random.normal(ks[8], (GEO_DIM,), jnp.float32) * s, 'v_null': jax.random.normal(ks[9], (ATTN_DIM,), jnp.float32) * s}
    _L0_attn_in = _L0_attn_setup()

    def _L0_ffn_setup():
        import math
        import jax
        import jax.numpy as jnp
        import numpy as np
        B, T, D = (1, 256, 128)
        H, KV, DH = (16, 4, 64)
        E, TOPK, DFF = (32, 4, 128)
        WINDOW = 128
        EPS = 1e-05
        ROPE_BASE = 150000.0
        ROPE_SCALE = 32.0

        def _rmsnorm(x, w):
            rms = jax.lax.rsqrt(jnp.mean(x * x, axis=-1, keepdims=True) + EPS)
            return w * (x * rms)

        def _apply_rope(x, sin, cos):
            x1, x2 = (x[..., ::2], x[..., 1::2])
            out = jnp.stack([x1 * cos - x2 * sin, x1 * sin + x2 * cos], axis=-1)
            return out.reshape(x.shape)
        key = jax.random.key(seed)
        ks = jax.random.split(key, 12)
        s = 0.02
        return {'x': jax.random.normal(ks[0], (B, T, D), jnp.float32), 'attn_norm_w': 1.0 + 0.02 * jax.random.normal(ks[1], (D,), jnp.float32), 'ffn_norm_w': 1.0 + 0.02 * jax.random.normal(ks[2], (D,), jnp.float32), 'qkv_w': s * jax.random.normal(ks[3], (D, H * DH + 2 * KV * DH), jnp.float32), 'qkv_b': s * jax.random.normal(ks[4], (H * DH + 2 * KV * DH,), jnp.float32), 'proj_w': s * jax.random.normal(ks[5], (H * DH, D), jnp.float32), 'proj_b': s * jax.random.normal(ks[6], (D,), jnp.float32), 'attn_sink': 0.5 * jax.random.normal(ks[7], (H,), jnp.float32), 'gate_w': s * jax.random.normal(ks[8], (D, E), jnp.float32), 'gate_b': s * jax.random.normal(ks[9], (E,), jnp.float32), 'W_up': s * jax.random.normal(ks[10], (E, D, 2 * DFF), jnp.float32), 'W_down': s * jax.random.normal(ks[11], (E, DFF, D), jnp.float32)}
    _L0_ffn_in = _L0_ffn_setup()
    _d = {'L0_attn_x': _L0_attn_in['x'], 'L0_attn_wq_sem': _L0_attn_in['wq_sem'], 'L0_attn_wk_sem': _L0_attn_in['wk_sem'], 'L0_attn_wq_geo': _L0_attn_in['wq_geo'], 'L0_attn_wk_geo': _L0_attn_in['wk_geo'], 'L0_attn_wv': _L0_attn_in['wv'], 'L0_attn_wo': _L0_attn_in['wo'], 'L0_attn_k_sem_null': _L0_attn_in['k_sem_null'], 'L0_attn_k_geo_null': _L0_attn_in['k_geo_null'], 'L0_attn_v_null': _L0_attn_in['v_null'], 'L0_ffn_attn_norm_w': _L0_ffn_in['attn_norm_w'], 'L0_ffn_ffn_norm_w': _L0_ffn_in['ffn_norm_w'], 'L0_ffn_qkv_w': _L0_ffn_in['qkv_w'], 'L0_ffn_qkv_b': _L0_ffn_in['qkv_b'], 'L0_ffn_proj_w': _L0_ffn_in['proj_w'], 'L0_ffn_proj_b': _L0_ffn_in['proj_b'], 'L0_ffn_attn_sink': _L0_ffn_in['attn_sink'], 'L0_ffn_gate_w': _L0_ffn_in['gate_w'], 'L0_ffn_gate_b': _L0_ffn_in['gate_b'], 'L0_ffn_W_up': _L0_ffn_in['W_up'], 'L0_ffn_W_down': _L0_ffn_in['W_down']}
    _x0 = _d['L0_attn_x']
    _d['L0_attn_x'] = jax.random.normal(jax.random.fold_in(jax.random.key(seed), 1), (8, 256, 128), dtype=_x0.dtype)
    del _x0
    return _d

def reference(L0_attn_x, L0_attn_wq_sem, L0_attn_wk_sem, L0_attn_wq_geo, L0_attn_wk_geo, L0_attn_wv, L0_attn_wo, L0_attn_k_sem_null, L0_attn_k_geo_null, L0_attn_v_null, L0_ffn_attn_norm_w, L0_ffn_ffn_norm_w, L0_ffn_qkv_w, L0_ffn_qkv_b, L0_ffn_proj_w, L0_ffn_proj_b, L0_ffn_attn_sink, L0_ffn_gate_w, L0_ffn_gate_b, L0_ffn_W_up, L0_ffn_W_down):

    def _L0_attn_ref(x, wq_sem, wk_sem, wq_geo, wk_geo, wv, wo, k_sem_null, k_geo_null, v_null):
        import jax, jax.numpy as jnp
        import numpy as np
        B, T, D = (1, 256, 128)
        H = 16
        SEM_DIM, GEO_DIM, ATTN_DIM = (64, 64, 128)
        ROPE_BASE = 10000.0
        NEG = -1000000000.0

        def _heads(y, hd):
            b, t, _ = y.shape
            return y.reshape(b, t, H, hd).transpose(0, 2, 1, 3)

        def _rope(x, cos, sin):
            hd = x.shape[-1]
            x1, x2 = (x[..., :hd // 2], x[..., hd // 2:])
            c = cos[None, None]
            sn = sin[None, None]
            return jnp.concatenate([x1 * c - x2 * sn, x2 * c + x1 * sn], axis=-1)

        def _forward(x, wq_sem, wk_sem, wq_geo, wk_geo, wv, wo, k_sem_null, k_geo_null, v_null):
            b, t, _ = x.shape
            sem_hd = wq_sem.shape[1] // H
            geo_hd = wq_geo.shape[1] // H
            v_hd = wv.shape[1] // H
            sem_scale = 1.0 / np.sqrt(sem_hd)
            geo_scale = 1.0 / np.sqrt(geo_hd)
            qs = _heads(x @ wq_sem, sem_hd)
            ks = _heads(x @ wk_sem, sem_hd)
            qg = _heads(x @ wq_geo, geo_hd)
            kg = _heads(x @ wk_geo, geo_hd)
            v = _heads(x @ wv, v_hd)
            pos = jnp.arange(t, dtype=jnp.float32)
            inv_freq = 1.0 / ROPE_BASE ** (jnp.arange(0, geo_hd, 2, dtype=jnp.float32) / geo_hd)
            ang = pos[:, None] * inv_freq[None, :]
            cos, sin = (jnp.cos(ang), jnp.sin(ang))
            qg = _rope(qg, cos, sin)
            kg = _rope(kg, cos, sin)
            ksn = jnp.broadcast_to(k_sem_null.reshape(1, 1, H, sem_hd).transpose(0, 2, 1, 3), (b, H, 1, sem_hd))
            kgn = jnp.broadcast_to(k_geo_null.reshape(1, 1, H, geo_hd).transpose(0, 2, 1, 3), (b, H, 1, geo_hd))
            vn = jnp.broadcast_to(v_null.reshape(1, 1, H, v_hd).transpose(0, 2, 1, 3), (b, H, 1, v_hd))
            ks_full = jnp.concatenate([ksn, ks], axis=2)
            kg_full = jnp.concatenate([kgn, kg], axis=2)
            v_full = jnp.concatenate([vn, v], axis=2)
            scores = jnp.einsum('bhqd,bhkd->bhqk', qs, ks_full).astype(jnp.float32) * sem_scale + jnp.einsum('bhqd,bhkd->bhqk', qg, kg_full).astype(jnp.float32) * geo_scale
            causal = jnp.tril(jnp.ones((t, t), dtype=bool))
            mask = jnp.concatenate([jnp.ones((t, 1), dtype=bool), causal], axis=1)
            scores = jnp.where(mask[None, None], scores, NEG)
            probs = jax.nn.softmax(scores, axis=-1).astype(v.dtype)
            out = jnp.einsum('bhqk,bhkd->bhqd', probs, v_full)
            out = out.transpose(0, 2, 1, 3).reshape(b, t, H * v_hd)
            return out @ wo
        return _forward(x, wq_sem, wk_sem, wq_geo, wk_geo, wv, wo, k_sem_null, k_geo_null, v_null)

    def _L0_ffn_ref(x, attn_norm_w, ffn_norm_w, qkv_w, qkv_b, proj_w, proj_b, attn_sink, gate_w, gate_b, W_up, W_down):
        import math
        import jax
        import jax.numpy as jnp
        import numpy as np
        B, T, D = (1, 256, 128)
        H, KV, DH = (16, 4, 64)
        E, TOPK, DFF = (32, 4, 128)
        WINDOW = 128
        EPS = 1e-05
        ROPE_BASE = 150000.0
        ROPE_SCALE = 32.0

        def _rmsnorm(x, w):
            rms = jax.lax.rsqrt(jnp.mean(x * x, axis=-1, keepdims=True) + EPS)
            return w * (x * rms)

        def _apply_rope(x, sin, cos):
            x1, x2 = (x[..., ::2], x[..., 1::2])
            out = jnp.stack([x1 * cos - x2 * sin, x1 * sin + x2 * cos], axis=-1)
            return out.reshape(x.shape)
        Bx, Tx, Dx = x.shape
        h = _rmsnorm(x, attn_norm_w)
        qkv = h @ qkv_w + qkv_b
        q = qkv[..., :H * DH].reshape(Bx, Tx, H, DH).transpose(0, 2, 1, 3)
        k = qkv[..., H * DH:H * DH + KV * DH].reshape(Bx, Tx, KV, DH).transpose(0, 2, 1, 3)
        v = qkv[..., H * DH + KV * DH:].reshape(Bx, Tx, KV, DH).transpose(0, 2, 1, 3)
        pos = jnp.arange(Tx, dtype=jnp.float32) / ROPE_SCALE
        inv_freq = 1.0 / ROPE_BASE ** (jnp.arange(0, DH, 2, dtype=jnp.float32) / DH)
        freqs = pos[:, None] * inv_freq[None, :]
        sin, cos = (jnp.sin(freqs), jnp.cos(freqs))
        q = _apply_rope(q, sin, cos)
        k = _apply_rope(k, sin, cos)
        rep = H // KV
        k = jnp.repeat(k, rep, axis=1)
        v = jnp.repeat(v, rep, axis=1)
        logits = jnp.einsum('bhqd,bhkd->bhqk', q, k) / math.sqrt(DH)
        i = jnp.arange(Tx)[:, None]
        j = jnp.arange(Tx)[None, :]
        mask = (j > i) | (i - j > WINDOW)
        logits = jnp.where(mask, -jnp.inf, logits)
        lse = jax.nn.logsumexp(logits, axis=-1, keepdims=True)
        denom_log = jnp.logaddexp(lse, attn_sink.reshape(1, H, 1, 1))
        attn = jnp.exp(logits - denom_log)
        y = jnp.einsum('bhqk,bhkd->bhqd', attn, v)
        y = y.transpose(0, 2, 1, 3).reshape(Bx, Tx, H * DH)
        x = x + (y @ proj_w + proj_b)
        h2 = _rmsnorm(x, ffn_norm_w).reshape(Bx * Tx, Dx)
        glogits = h2 @ gate_w + gate_b
        topv, topi = jax.lax.top_k(glogits, TOPK)
        gw = jax.nn.softmax(topv, axis=-1)
        N = Bx * Tx
        combine = jnp.zeros((N, E), x.dtype).at[jnp.arange(N)[:, None], topi].add(gw)

        def body(acc, we):
            wu, wd, ce = we
            ug = h2 @ wu
            u, g = (ug[:, :DFF], ug[:, DFF:])
            return (acc + ce[:, None] * (jax.nn.silu(g) * u @ wd), None)
        y2, _ = jax.lax.scan(body, jnp.zeros_like(h2), (W_up, W_down, combine.T))
        return x + y2.reshape(Bx, Tx, Dx)
    x = L0_attn_x
    x = x + 0.5 * _L0_ffn_ref(_layernorm(x, axis=-1), L0_ffn_attn_norm_w, L0_ffn_ffn_norm_w, L0_ffn_qkv_w, L0_ffn_qkv_b, L0_ffn_proj_w, L0_ffn_proj_b, L0_ffn_attn_sink, L0_ffn_gate_w, L0_ffn_gate_b, L0_ffn_W_up, L0_ffn_W_down)
    x = x + _L0_attn_ref(_layernorm(x, axis=-1), L0_attn_wq_sem, L0_attn_wk_sem, L0_attn_wq_geo, L0_attn_wk_geo, L0_attn_wv, L0_attn_wo, L0_attn_k_sem_null, L0_attn_k_geo_null, L0_attn_v_null)
    x = x + 0.5 * _L0_ffn_ref(_layernorm(x, axis=-1), L0_ffn_attn_norm_w, L0_ffn_ffn_norm_w, L0_ffn_qkv_w, L0_ffn_qkv_b, L0_ffn_proj_w, L0_ffn_proj_b, L0_ffn_attn_sink, L0_ffn_gate_w, L0_ffn_gate_b, L0_ffn_W_up, L0_ffn_W_down)
    return x

_drawn_inputs = setup_inputs


def setup_inputs(seed=0):
    import zlib

    import numpy as np

    out = dict(_drawn_inputs(seed))
    spreads = {}
    factors = {'L0_attn_wq_sem': 8.0,
     'L0_attn_wk_sem': 8.0,
     'L0_attn_wq_geo': 8.0,
     'L0_attn_wk_geo': 8.0,
     'L0_attn_wv': 8.0,
     'L0_attn_wo': 8.0,
     'L0_attn_k_sem_null': 64.0,
     'L0_attn_k_geo_null': 64.0,
     'L0_attn_v_null': 64.0,
     'L0_ffn_attn_norm_w': 8.0,
     'L0_ffn_ffn_norm_w': 8.0,
     'L0_ffn_qkv_w': 4.98,
     'L0_ffn_qkv_b': 7.824,
     'L0_ffn_proj_w': 4.292,
     'L0_ffn_proj_b': 4.541,
     'L0_ffn_attn_sink': 8.0,
     'L0_ffn_gate_w': 8.0,
     'L0_ffn_gate_b': 8.0,
     'L0_ffn_W_up': 8.0,
     'L0_ffn_W_down': 8.0}
    for name, (base, spread) in spreads.items():
        noise = np.random.default_rng([zlib.crc32(name.encode()), seed]).standard_normal(out[name].shape)
        drawn = base * np.exp(spread * noise) if base else spread * noise
        out[name] = jnp.asarray(drawn.astype(out[name].dtype))
    for name, factor in factors.items():
        out[name] = (out[name] * factor).astype(out[name].dtype)
    return out
```

```python
import math
from contextlib import ExitStack

import numpy as np

import concourse.bass as bass
from concourse import mybir

ACT = mybir.ActivationFunctionType
ALU = mybir.AluOpType
AX = mybir.AxisListType
F32 = mybir.dt.float32
F32R = mybir.dt.float32r
BF16 = mybir.dt.bfloat16
U32 = mybir.dt.uint32

BATCH, T, D = 8, 256, 128
P = 128
TILES = BATCH * T // P
TOKENS = BATCH * T
H = 16
G = 4
KV, DH = 4, 64
QB = H * DH // P
KB = KV * DH // P
HD = 4
VD = 8
E, TOPK, DFF = 32, 4, 128
WINDOW = 128
EPS = 1e-5
MASKED = -1e30

ROUNDS = BATCH // 2
UNITS = 2 * 2 * 4
CHUNKS = TOKENS // 512

W_QK, W_SWAP = 0, (QB + KB) * P
W_V = 2 * (QB + KB) * P
W_PROJ = W_V + KV * DH
W_GATE = W_PROJ + QB * D
W_END = W_GATE + E
M_Q, M_QS, M_K, M_KS, M_V, M_O, M_END = (P * i for i in range(7))
C_B, C_BS, C_W1, C_W2, C_NULL, C_END = 0, QB + KB, 2 * (QB + KB), 2 * (QB + KB) + 1, 2 * (QB + KB) + 2, 2 * (QB + KB) + 3
R_BV = 0
R_PB = R_BV + KV * DH
R_SINK = R_PB + D
R_GB = R_SINK + H
R_VN = R_GB + E
R_END = R_VN + P
T_FFN, T_MID = 0, 4 * T
T_ID = 8 * T
T_HEAD = T_ID + P
T_IOTA = T_HEAD + H
T_END = T_IOTA + E
B_ID, B_M0, B_M1F, B_M1M, B_END = 0, P, P + 512, P + 1024, P + 1536


def shape_constants():
    f32 = np.float32
    pos = np.arange(T, dtype=f32)

    def rotary(angle, scale, signs):
        return [f32(scale) * np.cos(angle), f32(scale) * np.sin(angle) * signs]

    inv = (f32(1.0) / f32(150000.0) ** (np.arange(0, DH, 2, dtype=f32) / f32(DH))).astype(f32)
    angle = ((pos / f32(32.0))[None, :] * inv[:, None]).astype(f32)
    dim = np.arange(P) % DH
    angle = angle[dim // 2]
    sign = np.where(dim % 2 == 0, -1.0, 1.0).astype(f32)[:, None]
    ffn = rotary(angle, DH ** -0.5, sign) + rotary(angle, 1.0, sign)

    inv = (f32(1.0) / f32(10000.0) ** (np.arange(0, HD, 2, dtype=f32) / f32(HD))).astype(f32)
    angle = (pos[None, :] * inv[:, None]).astype(f32)
    dim = np.arange(P // 2) % HD
    angle = np.concatenate([np.zeros((P // 2, T), f32), angle[dim % (HD // 2)]])
    sign = np.concatenate([np.ones(P // 2), np.where(dim < HD // 2, -1.0, 1.0)]).astype(f32)[:, None]
    mid = rotary(angle, HD ** -0.5, sign) + rotary(angle, 1.0, sign)

    head = (np.arange(P)[:, None] % (P // 2) // HD == np.arange(H)[None, :]).astype(f32)
    iota = np.tile(np.arange(E, dtype=f32), (P, 1))
    table = np.concatenate(ffn + mid + [np.eye(P, dtype=f32), head, iota], axis=1)

    query, key = np.arange(P)[:, None], np.arange(P)[None, :]
    future = np.where(key > query, MASKED, 0.0)
    stale = np.where(P + query - key > WINDOW, MASKED, 0.0)
    none = np.zeros((P, P))
    masks = [np.eye(P)] + [future] * 4 + [stale, future] * 2 + [none, future] * 2
    return np.ascontiguousarray(table, dtype=f32), np.concatenate(masks, axis=1).astype(np.dtype("bfloat16"))



class Signals:

    def __init__(self, sems, past):
        self.sems, self.past = sems, past

    def __getitem__(self, name):
        return self.sems[name]

    def at(self, name, value):
        return self.sems[name], value + self.past[name]


ATTENTION_SIGNALS = dict(
    stats=(2, 2), moments=(2, 2), pow_ready=(2, 1), rstd=(1, 1), xn_ready=(2, 0), normed=(2, 2), xT_ready=(1, 1),
    misc_full=(25, 11), misc_free=(25, 11), ab_ready=(20, 4), q_ready=(8, 1), kT_ready=(0, 1), k_ready=(2, 4),
    v_ready=(2, 2), null_ready=(0, 2), scores_full=(8, 8), rowmax=(8, 8), shift_ready=(8, 8), exp_done=(8, 8),
    pT_full=(8, 8), pT_ready=(8, 8), pT1_ready=(4, 4), y_full=(8, 8), yraw_ready=(8, 8), sink_shift=(2, 2),
    sink_exp=(2, 2), denom=(2, 2), rinv_ready=(2, 2), null_step=(0, 4), yn_ready=(2, 2), yT_ready=(4, 2),
    base_ready=(1, 0), x1_ready=(2, 2), square_ready=(2, 0), rms_step=(4, 0), h2_ready=(2, 0), h2T_ready=(2, 0),
    h2_split=(4, 0), gate_step=(10, 0), top_shift=(2, 0), top_exp=(2, 0), top_weight=(4, 0), combine_ready=(2, 0),
    cT_ready=(2, 0))
PRIMED = ("exp_done", "pT_ready", "pT1_ready", "yraw_ready", "scores_full", "y_full", "x1_ready", "h2_split")
EXPERT_SIGNALS = dict(
    combine_out=16, w_loaded0=8 * E, w_loaded1=8 * E, d_loaded0=8 * E, d_loaded1=8 * E, cb_loaded0=8 * E,
    cb_loaded1=8 * E, w_high=E, w_low=E, ug_full=CHUNKS * E,
    sg_ready=CHUNKS * E, hu_ready=CHUNKS * E, h_ready=CHUNKS * E, down_done=CHUNKS * E, y2T_ready=CHUNKS,
    turn_full=TILES, turn_free=TILES)


class Layer:

    def __init__(self, ffn, signals):
        self.ffn, self.signals = ffn, signals
        self.blocks = QB if ffn else 1
        self.ropes = QB + KB if ffn else 2
        self.width = DH if ffn else VD
        self.values = KV * DH if ffn else P
        self.turns = 2 if ffn else 1
        rope = [("rope", i) for i in range(self.ropes)]
        value = [("value", 0), ("value", 1)]
        self.front = [("turn_x", 0)] + rope + value + ([] if ffn else [("null", 0), ("null", 1)])
        if ffn:
            at = {1: [1] + [2 + i // 2 for i in range(12)],
                  2: [13] + [14 + i * 9 // 12 for i in range(12)]}
        else:
            at = {1: [1, 2, 2, 3, 3, 4, 4], 2: [13, 14, 14, 15, 15, 16, 16]}
        self.norm_slot = {1: 0, 2: 11}
        self.slots = 25 if ffn else 21
        self.steps = [[] for _ in range(self.slots)]
        for ahead in (1, 2):
            for step, slot in zip(self.front, at[ahead]):
                self.steps[slot].append((ahead,) + step)
        for lt in range(4):
            for part in range(self.turns):
                self.steps[4 * lt + 7].append((0, "turn_y", (lt, part)))
            self.steps[4 * lt + 8].append((0, "project", lt))
            if ffn:
                self.steps[4 * lt + 10].append((0, "turn_h", lt))
                self.steps[4 * lt + 11].append((0, "gate", lt))
                self.steps[4 * lt + 12].append((0, "turn_c", lt))
        self.order = {}
        for last in (False, True):
            flat = [step for slot in range(self.slots) for step in self.misc(slot, last)]
            self.order[last] = {step: n for n, step in enumerate(flat)}

    def misc(self, slot, last):
        return [step for step in self.steps[slot] if not (last and step[0] == 2)]

    def use(self, k, last, step):
        return len(self.front) + len(self.order[False]) * k + self.order[last][step]


def build(nc, x, table, masks, ffn_w, mid_w, columns, rows, w_up, w_down, out):
    combine_dram = [nc.dram_tensor(f"combine_{n}", (E, TOKENS), F32).ap() for n in range(2)]
    with ExitStack() as ctx:
        def sb(name, shape, dt=F32):
            return ctx.enter_context(nc.sbuf_tensor(name, shape, dt))

        def sem(name):
            return ctx.enter_context(nc.semaphore(name))

        ps = ctx.enter_context(nc.psum_tensor("ps", [P, 8, 512], F32))
        BANK_PT, BANK_Y, BANK_MISC = 4, 6, 7
        BANK_U, BANK_G, BANK_ACC = 0, 2, 4
        misc = ps[:, BANK_MISC, :]

        xr = sb("xr", [P, TILES * D])
        tb = sb("tb", [P, T_END])
        mk = sb("mk", [P, B_END], BF16)
        wf = sb("wf", [P, W_END])
        wm = sb("wm", [P, M_END])
        col = sb("col", [P, C_END])
        row = sb("row", [P, R_END])
        ident = tb[:, T_ID:T_ID + P]
        head_mask = tb[:, T_HEAD:T_HEAD + H]
        iota = tb[:, T_IOTA:T_IOTA + E]
        neg_sink = sb("neg_sink", [P, H])
        null_q = sb("null_q", [P, H])
        bf_zero = sb("bf_zero", [P, 512], BF16)
        stat = sb("stat", [P, 2, 6])
        mv = sb("mv", [P, 2, 2])
        powers = sb("powers", [P, 2, 2])
        rstd = sb("rstd", [P, 2, 2])
        minus_half = sb("minus_half", [P, 4])
        eps = sb("eps", [P, 1])
        xn = sb("xn", [P, 2, D])
        hh = sb("hh", [P, 2, D])
        base = sb("base", [P, 2, 2, D])
        xT = sb("xT", [P, T])
        rot_a = sb("rot_a", [P, 2, T])
        rot_b = sb("rot_b", [P, 2, T])
        qT = sb("qT", [P, 2, QB, T])
        kpad = sb("kpad", [P, 2, KV, 2, T])
        shared = sb("shared", [P, 2 * H * T])
        kz = shared[:, :].rearrange("p (s h t) -> p s h t", s=2, h=H)
        kT = sb("kT", [P, T])
        v = sb("v", [P, 2, 2, KV * DH])
        neg_null = sb("neg_null", [P, 2, 2, H])
        prob = sb("prob", [P, 2, 4, T])
        pT = sb("pT", [P, 2, 2, 512])
        top1 = sb("top1", [P, 2, 4])
        shift = sb("shift", [P, 2, H])
        total = sb("total", [P, 2, H])
        sshift = sb("sshift", [P, 2, H])
        sexp = sb("sexp", [P, 2, H])
        denom = sb("denom", [P, 2, H])
        rinv = sb("rinv", [P, 2, H])
        yraw = sb("yraw", [P, 2, H * DH])
        nully = sb("nully", [P, P])
        yn = sb("yn", [P, H * DH])
        yT = sb("yT", [P, H * DH])
        x1 = sb("x1", [P, D])
        junk = sb("junk", [P, D])
        msq = sb("msq", [P, 1])
        msq_eps = sb("msq_eps", [P, 1])
        rms = sb("rms", [P, 1])
        h2 = sb("h2", [P, D])
        h2T = sb("h2T", [P, P])
        h2h = sb("h2h", [P, TOKENS], F32R)
        h2l = sb("h2l", [P, TOKENS], F32R)
        gl = sb("gl", [P, E])
        top8 = sb("top8", [P, 8])
        idx = sb("idx", [P, 8], U32)
        idxf = sb("idxf", [P, 8])
        ntop = sb("ntop", [P, 1])
        etop = sb("etop", [P, TOPK])
        esum = sb("esum", [P, 1])
        rsum = sb("rsum", [P, 1])
        wtop = sb("wtop", [P, TOPK])
        picks = sb("picks", [P, TOPK, E])
        comb = sb("comb", [P, E])
        cT = sb("cT", [E, TOKENS])
        up = sb("up", [P, 2, 2 * DFF])
        uph = sb("uph", [P, 2, 2 * DFF], F32R)
        upl = sb("upl", [P, 2, 2 * DFF], F32R)
        down = sb("down", [P, 2, D])
        sg = sb("sg", [P, 2, 512])
        cb = shared[:, 0:2 * TOKENS].rearrange("p (s t) -> p s t", s=2)
        hu = shared[:, 2 * TOKENS:3 * TOKENS].rearrange("p (n t) -> p n t", n=4)
        he = shared[:, 3 * TOKENS:4 * TOKENS].rearrange("p (n t) -> p n t", n=4)
        y2T = cb[:, 0, :]

        loaded = sem("loaded")
        prep = sem("prep")
        phase_done = sem("phase_done")
        stored = sem("stored")
        mid_sems = {s: sem(f"mid_{s}") for s, n in ATTENTION_SIGNALS.items() if n[1]}
        ffn_sems = {s: sem(f"ffn_{s}") for s, n in ATTENTION_SIGNALS.items() if n[0]}
        expert_sems = {s: sem(f"expert_{s}") for s in EXPERT_SIGNALS}
        layers = [Layer(True, Signals(ffn_sems, {s: int(s in PRIMED) for s in ffn_sems})),
                  Layer(False, Signals(mid_sems, {s: int(s in PRIMED) for s in mid_sems})),
                  Layer(True, Signals(ffn_sems, {s: int(s in PRIMED) + BATCH * ATTENTION_SIGNALS[s][0]
                                                 for s in ffn_sems}))]
        moe = [Signals(expert_sems, {s: 0 for s in expert_sems}), Signals(expert_sems, EXPERT_SIGNALS)]
        LOADS = 7
        ENGINES = 5
        PHASES = ("ffn0", "experts0", "mid", "ffn1", "experts1")

        def phase(eng, n):
            eng.drain().then_inc(phase_done, 1)
            eng.wait_ge(phase_done, ENGINES * (n + 1))

        def program(eng, attention, experts):
            attention(layers[0])
            phase(eng, 0)
            experts(0)
            phase(eng, 1)
            attention(layers[1])
            phase(eng, 2)
            attention(layers[2])
            phase(eng, 3)
            experts(1)

        def rounds(eng, body):
            with eng.Fori(0, ROUNDS - 1) as k:
                body(k, False)
            body(ROUNDS - 1, True)

        def misc_steps(L, k, s, last, place, front_step, tail_step):
            todo = L.misc(s, last)
            for step in (todo[0:1], todo[1:2], todo[2:])[place]:
                ahead, kind, arg = step
                if ahead:
                    front_step(2 * k + ahead, ahead % 2, L.use(k, last, step), kind, arg)
                else:
                    tail_step(k, L.use(k, last, step), kind, arg)

        def later(b):
            return not (isinstance(b, int) and b == 0)

        def keys(lt):
            return P * (lt % 2 + 1)

        def score_view(n, lt):
            if lt % 2 == 0:
                return ps[:, 2 * (n % 2), :].rearrange("p (h k) -> p h k", h=4)
            return ps[:, 2 * (n % 2):2 * (n % 2) + 2, :].rearrange("p b (h k) -> p (b h) k", h=2)

        block = ctx.enter_context(nc.Block())

        @block.sync
        def _(sp):
            sp.dma_start(xr[:, :].rearrange("p (c d) -> p c d", d=D),
                         x.rearrange("b (t p) d -> p (b t) d", p=P)).then_inc(loaded, 16)
            sp.dma_start(tb[:, :], table).then_inc(loaded, 16)
            sp.dma_start(col[:, :], columns).then_inc(loaded, 16)
            sp.dma_start(row[:, :], rows.broadcast_to([P, R_END])).then_inc(loaded, 16)
            sp.dma_start(wf[:, :], ffn_w).then_inc(loaded, 16)
            sp.dma_start(mk[:, :], masks).then_inc(loaded, 16)
            sp.dma_start(wm[:, :], mid_w).then_inc(loaded, 16)

            def attention(L):
                pass

            def experts(number):
                S = moe[number]
                dram = combine_dram[number]
                sp.dma_start(dram, cT[:, :]).then_inc(S["combine_out"], 16)

                def load(e, s, first):
                    if not first:
                        sp.wait_ge(*S.at("down_done", CHUNKS * (e - 1)))
                    sp.wait_ge(*S.at("combine_out", 16))
                    sp.dma_start(up[:, s, :], w_up[bass.ds(e, 1), :, :].rearrange("e d f -> d (e f)"))\
                        .then_inc(S[f"w_loaded{s}"], 16)
                    sp.dma_start(down[:, s, :], w_down[bass.ds(e, 1), :, :].rearrange("e f d -> f (e d)"))\
                        .then_inc(S[f"d_loaded{s}"], 16)
                    sp.dma_start(cb[:, s, :], dram[bass.ds(e, 1), :].broadcast_to([P, TOKENS]))\
                        .then_inc(S[f"cb_loaded{s}"], 16)

                load(0, 0, True)
                load(1, 1, True)
                with sp.Fori(1, E // 2) as kk:
                    for s in range(2):
                        load(kk * 2 + s, s, False)

            program(sp, attention, experts)
            sp.wait_ge(*moe[1].at("turn_free", TILES))
            sp.dma_start(out.rearrange("b (t p) d -> p (b t) d", p=P),
                         xr[:, :].rearrange("p (c d) -> p c d", d=D)).then_inc(stored, 16)
            sp.wait_ge(stored, 16)

        @block.tensor
        def _(pe):
            pe.wait_ge(loaded, 16 * LOADS)
            pe.wait_ge(prep, 6)

            def attention(L):
                S = L.signals

                def front_step(b, par, use, kind, i):
                    pe.wait_ge(*S.at("misc_free", use))
                    if kind == "turn_x":
                        pe.wait_ge(*S.at("normed", 2 * b + 2))
                        for t in range(2):
                            last = pe.transpose(misc[:, t * P:(t + 1) * P], (hh if L.ffn else xn)[:, t, :], ident)
                    elif kind == "rope":
                        pe.wait_ge(*S.at("xT_ready", b + 1))
                        if L.ffn:
                            blk = QB + i if i < KB else i - KB
                            pair = wf[:, W_QK + blk * P:], wf[:, W_SWAP + blk * P:]
                        else:
                            pair = ((wm[:, M_K:], wm[:, M_KS:]), (wm[:, M_Q:], wm[:, M_QS:]))[i]
                        for n, w in enumerate(pair):
                            last = pe.matmul(misc[:, n * T:(n + 1) * T], w[:, 0:P], xT[:, :], start=True, stop=True)
                    elif kind == "value":
                        w = wf[:, W_V:W_V + KV * DH] if L.ffn else wm[:, M_V:M_V + P]
                        last = pe.matmul(misc[:, 0:L.values], xT[:, i * P:(i + 1) * P], w, start=True, stop=True)
                    elif kind == "null":
                        pe.wait_ge(*S.at("q_ready", b + 1))
                        last = pe.matmul(misc[:, 0:H], qT[:, par, 0, i * P:(i + 1) * P], null_q[:, :],
                                         start=True, stop=True)
                    last.then_inc(S["misc_full"], 1)

                def tail_step(k, use, kind, arg):
                    lt = arg[0] if kind == "turn_y" else arg
                    tile = 4 * k + lt
                    pe.wait_ge(*S.at("misc_free", use))
                    if kind == "turn_y":
                        pe.wait_ge(*S.at("yn_ready", tile + 1))
                        blocks = 4 if L.ffn else 1
                        for n in range(blocks):
                            c = (arg[1] * blocks + n) * P
                            last = pe.transpose(misc[:, n * P:(n + 1) * P], yn[:, c:c + P], ident)
                    elif kind == "project":
                        pe.wait_ge(*S.at("yT_ready", L.turns * (tile + 1)))
                        blocks = QB if L.ffn else 1
                        for n in range(blocks):
                            w = wf[:, W_PROJ + n * D:W_PROJ + (n + 1) * D] if L.ffn else wm[:, M_O:M_O + D]
                            last = pe.matmul(misc[:, 0:D], yT[:, n * P:(n + 1) * P], w,
                                             start=(n == 0), stop=(n == blocks - 1))
                    elif kind == "turn_h":
                        pe.wait_ge(*S.at("h2_ready", tile + 1))
                        last = pe.transpose(misc[:, 0:P], h2[:, :], ident)
                    elif kind == "gate":
                        pe.wait_ge(*S.at("h2T_ready", tile + 1))
                        last = pe.matmul(misc[:, 0:E], h2T[:, :], wf[:, W_GATE:W_GATE + E], start=True, stop=True)
                    elif kind == "turn_c":
                        pe.wait_ge(*S.at("combine_ready", tile + 1))
                        last = pe.transpose(misc[0:E, 0:P], comb[:, :], ident)
                    last.then_inc(S["misc_full"], 1)

                def scores(k, s):
                    b, j, lt, g = 2 * k + s // 8, s // 8, s // 4, s % 4
                    if s == 0:
                        pe.wait_ge(*S.at("exp_done", UNITS * k))
                    elif s > 1:
                        pe.wait_ge(*S.at("exp_done", UNITS * k + s - 1))
                    if L.ffn:
                        pe.wait_ge(*S.at("q_ready", QB * b + 2 * g + 2))
                        pe.wait_ge(*S.at("k_ready", KB * b + g // 2 + 1))
                    else:
                        pe.wait_ge(*S.at("q_ready", b + 1))
                        pe.wait_ge(*S.at("k_ready", G * b + g + 1))
                    bank = 2 * (s % 2)
                    q0 = (lt % 2) * P
                    for n in range(2):
                        blk = 2 * g + n if L.ffn else 0
                        q = qT[:, j, blk, q0:q0 + P]
                        heads = kpad[:, j, g, :, 0:keys(lt)] if L.ffn else \
                            kz[:, j, 4 * g + 2 * n:4 * g + 2 * n + 2, 0:keys(lt)]
                        if lt % 2 == 0:
                            if n == 0:
                                pe.matmul(ps[:, bank, :], mk[:, B_ID:B_ID + P], mk[:, B_M0:B_M0 + 512],
                                          start=True, stop=False)
                            to = ps[:, bank, 256 * n:256 * n + 256]
                        else:
                            m = B_M1F if L.ffn else B_M1M
                            pe.matmul(ps[:, bank + n, :], mk[:, B_ID:B_ID + P], mk[:, m:m + 512],
                                      start=True, stop=False)
                            to = ps[:, bank + n, :]
                        last = pe.matmul(to.rearrange("p (h k) -> p h k", h=2), q, heads, start=False,
                                         stop=(lt % 2 == 1 or n == 1))
                    last.then_inc(S["scores_full"], 1)

                def turn_probs(k, s):
                    lt = s // 4
                    pe.wait_ge(*S.at("exp_done", UNITS * k + s + 1))
                    pe.wait_ge(*S.at("pT_ready", UNITS * k + s))
                    if lt > 0:
                        pe.wait_ge(*S.at("pT1_ready", UNITS // 2 * k + 4 * (lt // 2) + (s % 4 if lt % 2 else 0)))
                    for c in range(keys(lt) // P):
                        for h in range(4):
                            last = pe.transpose(ps[:, BANK_PT + c, h * P:(h + 1) * P],
                                                prob[:, s % 2, h, c * P:(c + 1) * P], ident)
                    last.then_inc(S["pT_full"], 1)

                def weigh(k, s):
                    b, j, lt, g = 2 * k + s // 8, s // 8, s // 4, s % 4
                    pe.wait_ge(*S.at("pT_ready", UNITS * k + s + 1))
                    if lt % 2:
                        pe.wait_ge(*S.at("pT1_ready", G * b + g + 1))
                    pe.wait_ge(*S.at("v_ready", 2 * b + 1 + lt % 2))
                    pe.wait_ge(*S.at("yraw_ready", UNITS * k + s))
                    w = L.width
                    for h in range(4):
                        for c in range(keys(lt) // P):
                            at = g * DH if L.ffn else (4 * g + h) * VD
                            last = pe.matmul(ps[:, BANK_Y, h * w:(h + 1) * w], pT[:, s % 2, c, h * P:(h + 1) * P],
                                             v[:, j, c, at:at + w], start=(c == 0), stop=(c == lt % 2))
                    last.then_inc(S["y_full"], 1)

                for n, step in enumerate(L.front):
                    front_step(0, 0, n, *step)

                def body(k, last):
                    for s in range(L.slots):
                        if s < UNITS:
                            scores(k, s)
                        misc_steps(L, k, s, last, 0, front_step, tail_step)
                        if 1 <= s <= UNITS:
                            turn_probs(k, s - 1)
                        misc_steps(L, k, s, last, 1, front_step, tail_step)
                        if 2 <= s <= UNITS + 1:
                            weigh(k, s - 2)
                        misc_steps(L, k, s, last, 2, front_step, tail_step)

                rounds(pe, body)

            def experts(number):
                S = moe[number]
                zero = bf_zero
                for c in range(CHUNKS):
                    last = pe.matmul(ps[:, BANK_ACC + c, :], zero[:, 0:P], zero[:, :], start=True, stop=False,
                                     skip_group_check=True)

                def ups(kk, j, wait):
                    e, s, c, two = kk * 2 + j // 4, j // 4 % 2, j % 4, j % 2
                    if c == 0:
                        pe.wait_ge(*S.at("w_low", e + 1))
                    if wait:
                        pe.wait_ge(*S.at("hu_ready", 8 * kk + j - 1))
                    xs = slice(512 * c, 512 * c + 512)
                    for n, bank in enumerate((BANK_U, BANK_G)):
                        f = slice(n * DFF, (n + 1) * DFF)
                        to = ps[:, bank + two, :]
                        pe.matmul(to, uph[:, s, f], h2h[:, xs], start=True, stop=False)
                        pe.matmul(to, uph[:, s, f], h2l[:, xs], start=False, stop=False)
                        last = pe.matmul(to, upl[:, s, f], h2h[:, xs], start=False, stop=True)
                    last.then_inc(S["ug_full"], 1)

                def downs(kk, j, final):
                    e, s, c = kk * 2 + j // 4, j // 4, j % 4
                    if c == 0:
                        pe.wait_ge(*S.at(f"d_loaded{s}", (kk + 1) * 16))
                    pe.wait_ge(*S.at("h_ready", 8 * kk + j + 1))
                    pe.matmul(ps[:, BANK_ACC + c, :], down[:, s, :], he[:, j % 4, :], start=False, stop=final,
                              skip_group_check=True).then_inc(S["down_done"], 1)

                ups(0, 0, False)
                ups(0, 1, False)

                def body(kk, last):
                    for j in range(8):
                        if not (last and j >= 6):
                            ups(kk, j + 2, True)
                        downs(kk, j, last and j >= 4)

                with pe.Fori(0, E // 2 - 1) as kk:
                    body(kk, False)
                body(E // 2 - 1, True)
                for n in range(TILES):
                    pe.wait_ge(*S.at("y2T_ready", n // 4 + 1))
                    if n >= 4:
                        pe.wait_ge(*S.at("turn_free", n - 3))
                    pe.transpose(ps[:, n % 4, 0:P], y2T[:, n * P:(n + 1) * P], ident).then_inc(S["turn_full"], 1)

            program(pe, attention, experts)

        @block.vector
        def _(dve):
            for sems in (ffn_sems, mid_sems):
                for name in PRIMED:
                    if name in sems:
                        dve.sem_inc(sems[name], 1)
            dve.memset(kpad[:, :, :, :, :], 0.0).then_inc(prep, 1)
            dve.memset(bf_zero[:, :], 0.0).then_inc(prep, 1)
            dve.wait_ge(loaded, 16 * LOADS)
            dve.tensor_scalar(neg_sink[:, :], row[:, R_SINK:R_SINK + H], -1.0, None, ALU.mult).then_inc(prep, 1)
            dve.tensor_scalar(null_q[:, :], head_mask, col[:, C_NULL:C_NULL + 1], None, ALU.mult).then_inc(prep, 1)
            dve.memset(eps[:, :], EPS).then_inc(prep, 1)
            dve.memset(minus_half[:, :], -0.5).then_inc(prep, 1)
            dve.wait_ge(prep, 6)

            def attention(L):
                S = L.signals

                def statistics(b):
                    for t in range(2):
                        xt = xr[:, bass.ds(b * T + t * P, P)]
                        dve.bn_stats(stat[:, t, :], xt).then_inc(S["stats"], 1)

                def moments(b):
                    for t in range(2):
                        dve.bn_aggr(mv[:, t, :], stat[:, t, :]).then_inc(S["moments"], 1)
                    dve.wait_ge(*S.at("moments", 2 * b + 2))
                    dve.tensor_scalar(powers[:, 0, :], mv[:, :, 1], EPS, None, ALU.add).then_inc(S["pow_ready"], 1)
                    if L.ffn:
                        dve.tensor_scalar(powers[:, 1, :], mv[:, :, 1], 1.0 + EPS, EPS * EPS, ALU.mult, ALU.add)\
                            .then_inc(S["pow_ready"], 1)

                def norm(b):
                    dve.wait_ge(*S.at("rstd", b + 1))
                    if later(b):
                        dve.wait_ge(*S.at("xT_ready", b))
                        if L.ffn:
                            dve.wait_ge(*S.at("base_ready", b))
                    for t in range(2):
                        xt = xr[:, bass.ds(b * T + t * P, P)]
                        dve.tensor_scalar(xn[:, t, :], xt, mv[:, t, 0:1], rstd[:, 0, t:t + 1], ALU.subtract,
                                          ALU.mult).then_inc(S["xn_ready" if L.ffn else "normed"], 1)
                    if L.ffn:
                        for t in range(2):
                            xt = xr[:, bass.ds(b * T + t * P, P)]
                            dve.tensor_scalar(hh[:, t, :], xt, mv[:, t, 0:1], rstd[:, 1, t:t + 1], ALU.subtract,
                                              ALU.mult).then_inc(S["normed"], 1)

                def front_step(b, par, use, kind, i):
                    if kind == "rope":
                        if L.ffn:
                            if i in (0, 1):
                                dve.wait_ge(*S.at("q_ready", QB * b))
                            elif i >= 4:
                                dve.wait_ge(*S.at("q_ready", QB * b + i - 3))
                        else:
                            dve.wait_ge(*S.at("q_ready" if i else "kT_ready", b))
                        dve.wait_ge(*S.at("misc_full", use + 1))
                        is_key = i < (KB if L.ffn else 1)
                        t0 = (T_FFN if L.ffn else T_MID) + (2 * T if is_key else 0)
                        for n, to in enumerate((rot_a, rot_b)):
                            src, angle = misc[:, n * T:(n + 1) * T], tb[:, t0 + n * T:t0 + (n + 1) * T]
                            if L.ffn:
                                blk = QB + i if is_key else i - KB
                                bias = col[:, C_B + blk:C_B + blk + 1] if n == 0 else \
                                    col[:, C_BS + blk:C_BS + blk + 1]
                                dve.scalar_tensor_tensor(to[:, i % 2, :], src, bias, angle, ALU.add, ALU.mult)\
                                    .then_inc(S["ab_ready"], 1)
                            else:
                                dve.tensor_tensor(to[:, i, :], src, angle, ALU.mult).then_inc(S["ab_ready"], 1)
                        dve.wait_ge(*S.at("ab_ready", 2 * (L.ropes * b + i + 1)))
                        dve.sem_inc(S["misc_free"], 1)
                        if L.ffn and is_key:
                            dve.wait_ge(*S.at("scores_full", 8 * (b - 1) if later(b) else 0))
                            for half in range(2):
                                src = slice(64 * half, 64 * half + 64)
                                for place in range(2):
                                    dst = slice(64 * place, 64 * place + 64)
                                    last = dve.tensor_tensor(kpad[dst, par, 2 * i + half, place, :],
                                                             rot_a[src, i, :], rot_b[src, i, :], ALU.add)
                            last.then_inc(S["k_ready"], 1)
                    elif kind == "value":
                        dve.wait_ge(*S.at("misc_full", use + 1))
                        if later(b):
                            dve.wait_ge(*S.at("y_full", 8 * (b - 1)))
                        if L.ffn:
                            dve.tensor_tensor(v[:, par, i, :], misc[:, 0:KV * DH], row[:, R_BV:R_BV + KV * DH],
                                              ALU.add).then_inc(S["v_ready"], 1)
                        else:
                            dve.tensor_copy(v[:, par, i, 0:P], misc[:, 0:P]).then_inc(S["v_ready"], 1)
                        dve.wait_ge(*S.at("v_ready", 2 * b + i + 1))
                        dve.sem_inc(S["misc_free"], 1)
                    elif kind == "null":
                        dve.wait_ge(*S.at("misc_full", use + 1))
                        dve.tensor_scalar(neg_null[:, par, i, :], misc[:, 0:H], -1.0, None, ALU.mult)\
                            .then_inc(S["null_ready"], 1)
                        dve.wait_ge(*S.at("null_ready", 2 * b + i + 1))
                        dve.sem_inc(S["misc_free"], 1)

                def negated(lt):
                    return neg_sink[:, :] if L.ffn else neg_null[:, lt // 2, lt % 2, :]

                def row_max(k, s):
                    lt, g = s // 4, s % 4
                    dve.wait_ge(*S.at("scores_full", UNITS * k + s + 1))
                    dve.tensor_reduce(top1[:, s % 2, :], score_view(s, lt), AX.X, ALU.max, negate=True)\
                        .then_inc(S["rowmax"], 1)
                    dve.wait_ge(*S.at("rowmax", UNITS * k + s + 1))
                    dve.tensor_tensor(shift[:, lt % 2, 4 * g:4 * g + 4], top1[:, s % 2, :],
                                      negated(lt)[:, 4 * g:4 * g + 4], ALU.min).then_inc(S["shift_ready"], 1)

                def copy_pT(k, s):
                    dve.wait_ge(*S.at("pT_full", UNITS * k + s + 1))
                    dve.tensor_copy(pT[:, s % 2, 0, :], ps[:, BANK_PT, :]).then_inc(S["pT_ready"], 1)

                def sink_shift(k, lt):
                    dve.wait_ge(*S.at("shift_ready", UNITS * k + 4 * lt + 4))
                    dve.tensor_tensor(sshift[:, lt % 2, :], shift[:, lt % 2, :], negated(lt), ALU.subtract)\
                        .then_inc(S["sink_shift"], 1)

                def normaliser(k, lt):
                    tile = 4 * k + lt
                    dve.wait_ge(*S.at("exp_done", UNITS * k + 4 * lt + 4))
                    dve.wait_ge(*S.at("sink_exp", tile + 1))
                    dve.tensor_tensor(denom[:, lt % 2, :], total[:, lt % 2, :], sexp[:, lt % 2, :], ALU.add)\
                        .then_inc(S["denom"], 1)
                    dve.wait_ge(*S.at("denom", tile + 1))
                    dve.reciprocal(rinv[:, lt % 2, :], denom[:, lt % 2, :]).then_inc(S["rinv_ready"], 1)

                def tail_step(k, use, kind, arg):
                    if kind not in ("project", "gate"):
                        return
                    lt = arg
                    tile = 4 * k + lt
                    xt = xr[:, bass.ds(tile * P, P)]
                    dve.wait_ge(*S.at("misc_full", use + 1))
                    if kind == "project" and L.ffn:
                        dve.tensor_tensor(x1[:, :], misc[:, 0:D], base[:, lt // 2, lt % 2, :], ALU.add)\
                            .then_inc(S["x1_ready"], 1)
                        dve.wait_ge(*S.at("x1_ready", tile + 1))
                        dve.sem_inc(S["misc_free"], 1)
                        dve.scalar_tensor_tensor(xt, x1[:, :], 0.5, xt, ALU.mult, ALU.add)
                    elif kind == "project":
                        dve.tensor_tensor(xt, misc[:, 0:D], xt, ALU.add).then_inc(S["x1_ready"], 1)
                        dve.wait_ge(*S.at("x1_ready", tile + 1))
                        dve.sem_inc(S["misc_free"], 1)
                    elif kind == "gate":
                        G0 = 5 * tile
                        dve.tensor_tensor(gl[:, :], misc[:, 0:E], row[:, R_GB:R_GB + E], ALU.add)\
                            .then_inc(S["gate_step"], 1)
                        dve.wait_ge(*S.at("gate_step", G0 + 1))
                        dve.sem_inc(S["misc_free"], 1)
                        dve.max(out=top8[:, :], in_=gl[:, :]).then_inc(S["gate_step"], 1)
                        dve.wait_ge(*S.at("gate_step", G0 + 2))
                        dve.tensor_scalar(ntop[:, :], top8[:, 0:1], -1.0, None, ALU.mult).then_inc(S["top_shift"], 1)
                        dve.max_index(out=idx[:, :], in_max=top8[:, :], in_values=gl[:, :])\
                            .then_inc(S["gate_step"], 1)
                        dve.wait_ge(*S.at("gate_step", G0 + 3))
                        dve.tensor_copy(idxf[:, :], idx[:, :]).then_inc(S["gate_step"], 1)

                def split_h2(k, lt):
                    tile = 4 * k + lt
                    high, low = h2h[:, bass.ds(tile * P, P)], h2l[:, bass.ds(tile * P, P)]
                    dve.wait_ge(*S.at("h2T_ready", tile + 1))
                    dve.tensor_copy(high, h2T[:, :]).then_inc(S["h2_split"], 1)
                    dve.wait_ge(*S.at("h2_split", 2 * tile + 1))
                    dve.tensor_tensor(low, h2T[:, :], high.bitcast(F32), ALU.subtract).then_inc(S["h2_split"], 1)

                def combine(k, lt):
                    tile = 4 * k + lt
                    dve.wait_ge(*S.at("top_exp", tile + 1))
                    dve.reciprocal(rsum[:, :], esum[:, :]).then_inc(S["top_weight"], 1)
                    dve.wait_ge(*S.at("top_weight", 2 * tile + 1))
                    dve.tensor_scalar(wtop[:, :], etop[:, :], rsum[:, 0:1], None, ALU.mult)\
                        .then_inc(S["top_weight"], 1)
                    dve.wait_ge(*S.at("top_weight", 2 * tile + 2))
                    dve.wait_ge(*S.at("gate_step", 5 * tile + 4))
                    for r in range(TOPK):
                        last = dve.tensor_scalar(picks[:, r, :], iota, idxf[:, r:r + 1], wtop[:, r:r + 1],
                                                 ALU.is_equal, ALU.mult)
                    last.then_inc(S["gate_step"], 1)
                    dve.wait_ge(*S.at("gate_step", 5 * tile + 5))
                    dve.tensor_reduce(comb[:, :], picks[:, :, :].rearrange("p r e -> p e r"), AX.X, ALU.add)\
                        .then_inc(S["combine_ready"], 1)

                statistics(0)
                dve.wait_ge(*S.at("stats", 2))
                moments(0)
                norm(0)
                for n, step in enumerate(L.front):
                    front_step(0, 0, n, *step)

                def body(k, last):
                    for s in range(L.slots):
                        for ahead in (1, 2):
                            if s == L.norm_slot[ahead] and not (last and ahead == 2):
                                statistics(2 * k + ahead)
                                dve.wait_ge(*S.at("stats", 2 * (2 * k + ahead) + 2))
                        if s < UNITS:
                            row_max(k, s)
                        for ahead in (1, 2):
                            if s == L.norm_slot[ahead] and not (last and ahead == 2):
                                moments(2 * k + ahead)
                            if s == L.norm_slot[ahead] + 1 and not (last and ahead == 2):
                                norm(2 * k + ahead)
                        for lt in range(4):
                            if s == 4 * lt + 4:
                                sink_shift(k, lt)
                            if s == 4 * lt + 5:
                                normaliser(k, lt)
                            if L.ffn and s == 4 * lt + 11:
                                split_h2(k, lt)
                            if L.ffn and s == 4 * lt + 12:
                                combine(k, lt)
                        misc_steps(L, k, s, last, 0, front_step, tail_step)
                        if 1 <= s <= UNITS:
                            copy_pT(k, s - 1)
                        misc_steps(L, k, s, last, 1, front_step, tail_step)
                        misc_steps(L, k, s, last, 2, front_step, tail_step)

                rounds(dve, body)

            def experts(number):
                S = moe[number]

                def split_low(e, s):
                    dve.wait_ge(*S.at("w_high", e + 1))
                    dve.tensor_tensor(upl[:, s, :], up[:, s, :], uph[:, s, :].bitcast(F32), ALU.subtract)\
                        .then_inc(S["w_low"], 1)

                def gated(kk, j):
                    dve.wait_ge(*S.at("sg_ready", 8 * kk + j + 1))
                    dve.tensor_tensor(hu[:, j % 4, :], ps[:, BANK_U + j % 2, :], sg[:, j % 2, :], ALU.mult)\
                        .then_inc(S["hu_ready"], 1)

                split_low(0, 0)

                def body(kk, last):
                    for j in range(8):
                        gated(kk, j)
                        if j == 1:
                            split_low(kk * 2 + 1, 1)
                        if j == 5 and not last:
                            split_low(kk * 2 + 2, 0)

                with dve.Fori(0, E // 2 - 1) as kk:
                    body(kk, False)
                body(E // 2 - 1, True)
                for c in range(2):
                    dve.wait_ge(*S.at("down_done", CHUNKS * (E - 1) + 2 * c + 2))
                    dve.tensor_copy(y2T[:, 1024 * c:1024 * c + 1024].rearrange("p (b t) -> p b t", b=2),
                                    ps[:, BANK_ACC + 2 * c:BANK_ACC + 2 * c + 2, :]).then_inc(S["y2T_ready"], 2)
                for n in range(TILES):
                    xt = xr[:, n * P:(n + 1) * P]
                    dve.wait_ge(*S.at("turn_full", n + 1))
                    dve.scalar_tensor_tensor(xt, ps[:, n % 4, 0:P], 0.5, xt, ALU.mult, ALU.add)\
                        .then_inc(S["turn_free"], 1)

            program(dve, attention, experts)

        @block.scalar
        def _(act):
            act.wait_ge(loaded, 16 * LOADS)
            act.wait_ge(prep, 6)

            def attention(L):
                S = L.signals

                def release(copied, value):
                    act.wait_ge(*S.at(copied, value))
                    act.sem_inc(S["misc_free"], 1)

                def front_step(b, par, use, kind, i):
                    if kind == "turn_x":
                        act.wait_ge(*S.at("misc_full", use + 1))
                        if L.ffn:
                            act.activation(xT[:, :], misc[:, 0:T], ACT.Copy, scale=col[:, C_W1:C_W1 + 1])\
                                .then_inc(S["xT_ready"], 1)
                        else:
                            act.activation(xT[:, :], misc[:, 0:T], ACT.Copy).then_inc(S["xT_ready"], 1)
                        release("xT_ready", b + 1)

                def exps(k, s):
                    lt, g = s // 4, s % 4
                    act.wait_ge(*S.at("shift_ready", UNITS * k + s + 1))
                    for h in range(4):
                        one = 4 * g + h
                        last = act.activation(prob[:, s % 2, h, 0:keys(lt)], score_view(s, lt)[:, h, :], ACT.Exp,
                                              bias=shift[:, lt % 2, one:one + 1],
                                              accum_out=total[:, lt % 2, one:one + 1])
                    last.then_inc(S["exp_done"], 1)

                def sink_exp(k, lt):
                    act.wait_ge(*S.at("sink_shift", 4 * k + lt + 1))
                    act.activation(sexp[:, lt % 2, :], sshift[:, lt % 2, :], ACT.Exp).then_inc(S["sink_exp"], 1)

                def copy_pT1(k, s):
                    act.wait_ge(*S.at("pT_full", UNITS * k + s + 1))
                    act.activation(pT[:, s % 2, 1, :], ps[:, BANK_PT + 1, :], ACT.Copy).then_inc(S["pT1_ready"], 1)

                def copy_y(k, s):
                    lt, g = s // 4, s % 4
                    act.wait_ge(*S.at("y_full", UNITS * k + s + 1))
                    n = 4 * L.width
                    act.activation(yraw[:, lt % 2, g * n:(g + 1) * n], ps[:, BANK_Y, 0:n], ACT.Copy)\
                        .then_inc(S["yraw_ready"], 1)

                def tail_step(k, use, kind, arg):
                    lt = arg[0] if kind == "turn_y" else arg
                    tile = 4 * k + lt
                    if kind == "turn_y":
                        n = 4 * P if L.ffn else P
                        act.wait_ge(*S.at("misc_full", use + 1))
                        act.activation(yT[:, arg[1] * n:(arg[1] + 1) * n], misc[:, 0:n], ACT.Copy)\
                            .then_inc(S["yT_ready"], 1)
                        release("yT_ready", L.turns * tile + arg[1] + 1)
                    elif kind == "project" and L.ffn:
                        act.wait_ge(*S.at("x1_ready", tile + 1))
                        act.activation(junk[:, :], x1[:, :], ACT.Square, scale=D ** -0.5, accum_out=msq[:, :])\
                            .then_inc(S["square_ready"], 1)
                    elif kind == "turn_h":
                        act.wait_ge(*S.at("misc_full", use + 1))
                        act.wait_ge(*S.at("h2_split", 2 * tile))
                        act.activation(h2T[:, :], misc[:, 0:P], ACT.Copy, scale=col[:, C_W2:C_W2 + 1])\
                            .then_inc(S["h2T_ready"], 1)
                        release("h2T_ready", tile + 1)
                    elif kind == "gate":
                        act.wait_ge(*S.at("top_shift", tile + 1))
                        act.activation(etop[:, :], top8[:, 0:TOPK], ACT.Exp, bias=ntop[:, :], accum_out=esum[:, :])\
                            .then_inc(S["top_exp"], 1)
                    elif kind == "turn_c":
                        act.wait_ge(*S.at("misc_full", use + 1))
                        act.activation(cT[:, bass.ds(tile * P, P)], misc[0:E, 0:P], ACT.Copy).then_inc(S["cT_ready"], 1)
                        release("cT_ready", tile + 1)

                for n, step in enumerate(L.front):
                    front_step(0, 0, n, *step)

                def body(k, last):
                    for s in range(L.slots):
                        if s < UNITS:
                            exps(k, s)
                        for lt in range(4):
                            if s == 4 * lt + 4:
                                sink_exp(k, lt)
                        misc_steps(L, k, s, last, 0, front_step, tail_step)
                        if 1 <= s <= UNITS and (s - 1) // 4 % 2:
                            copy_pT1(k, s - 1)
                        misc_steps(L, k, s, last, 1, front_step, tail_step)
                        if 2 <= s <= UNITS + 1:
                            copy_y(k, s - 2)
                        misc_steps(L, k, s, last, 2, front_step, tail_step)

                rounds(act, body)

            def experts(number):
                S = moe[number]

                def split_high(kk, s, wait):
                    act.wait_ge(*S.at(f"w_loaded{s}", (kk + 1) * 16))
                    if wait:
                        act.wait_ge(*S.at("ug_full", CHUNKS * (kk * 2 + s - 1)))
                    act.activation(uph[:, s, :], up[:, s, :], ACT.Copy).then_inc(S["w_high"], 1)

                def silu(kk, j):
                    act.wait_ge(*S.at("ug_full", 8 * kk + j + 1))
                    act.activation(sg[:, j % 2, :], ps[:, BANK_G + j % 2, :], ACT.Silu).then_inc(S["sg_ready"], 1)

                split_high(0, 0, False)
                split_high(0, 1, False)

                def body(kk, last):
                    for j in range(8):
                        silu(kk, j)
                        if j == 4 and not last:
                            split_high(kk + 1, 0, True)
                        if j == 7 and not last:
                            split_high(kk + 1, 1, True)

                with act.Fori(0, E // 2 - 1) as kk:
                    body(kk, False)
                body(E // 2 - 1, True)

            program(act, attention, experts)

        @block.gpsimd
        def _(pool):
            pool.wait_ge(loaded, 16 * LOADS)
            pool.wait_ge(prep, 6)

            def attention(L):
                S = L.signals

                def front_step(b, par, use, kind, i):
                    if kind == "turn_x" and L.ffn:
                        pool.wait_ge(*S.at("xn_ready", 2 * b + 2))
                        if later(b):
                            pool.wait_ge(*S.at("x1_ready", 2 * b - 2))
                        for t in range(2):
                            last = pool.tensor_tensor(base[:, par, t, :], xn[:, t, :], row[:, R_PB:R_PB + D], ALU.add)
                        last.then_inc(S["base_ready"], 1)
                    if kind == "rope" and L.ffn and i >= KB:
                        pool.wait_ge(*S.at("ab_ready", 2 * (L.ropes * b + i + 1)))
                        if later(b):
                            pool.wait_ge(*S.at("scores_full", 8 * (b - 1)))
                        pool.tensor_tensor(qT[:, par, i - KB, :], rot_a[:, i % 2, :], rot_b[:, i % 2, :], ALU.add)\
                            .then_inc(S["q_ready"], 1)
                    if kind == "rope" and not L.ffn:
                        pool.wait_ge(*S.at("ab_ready", 2 * (2 * b + i + 1)))
                        if later(b):
                            pool.wait_ge(*S.at("scores_full", 8 * (b - 1)))
                        if i == 0:
                            pool.tensor_tensor(kT[:, :], rot_a[:, 0, :], rot_b[:, 0, :], ALU.add)\
                                .then_inc(S["kT_ready"], 1)
                        else:
                            pool.tensor_tensor(qT[:, par, 0, :], rot_a[:, 1, :], rot_b[:, 1, :], ALU.add)\
                                .then_inc(S["q_ready"], 1)
                            pool.wait_ge(*S.at("kT_ready", b + 1))
                            for g in range(G):
                                shape = [P, 4, T]
                                pool.tensor_tensor(
                                    kz[:, par, 4 * g:4 * g + 4, :], kT[:, :].unsqueeze(1).broadcast_to(shape),
                                    head_mask[:, 4 * g:4 * g + 4].unsqueeze(2).broadcast_to(shape), ALU.mult)\
                                    .then_inc(S["k_ready"], 1)

                def tail_step(k, use, kind, arg):
                    pass

                def root(b):
                    n = 2 if L.ffn else 1
                    pool.wait_ge(*S.at("pow_ready", n * b + n))
                    if later(b):
                        pool.wait_ge(*S.at("normed", 2 * b))
                    pool.tensor_tensor(rstd[:, 0:n, :], powers[:, 0:n, :],
                                       minus_half[:, 0:2 * n].rearrange("p (n t) -> p n t", n=n), ALU.pow)\
                        .then_inc(S["rstd"], 1)

                def rms_norm(k, lt):
                    tile = 4 * k + lt
                    pool.wait_ge(*S.at("square_ready", tile + 1))
                    pool.tensor_tensor(msq_eps[:, :], msq[:, :], eps[:, :], ALU.add).then_inc(S["rms_step"], 1)
                    pool.wait_ge(*S.at("rms_step", 2 * tile + 1))
                    pool.tensor_tensor(rms[:, :], msq_eps[:, :], minus_half[:, 0:1], ALU.pow)\
                        .then_inc(S["rms_step"], 1)
                    pool.wait_ge(*S.at("rms_step", 2 * tile + 2))
                    pool.tensor_tensor(h2[:, :], x1[:, :], rms[:, 0:1].broadcast_to([P, D]), ALU.mult).then_inc(S["h2_ready"], 1)

                def normalise(k, lt):
                    tile = 4 * k + lt
                    w = L.width
                    shape = [P, H, w]
                    y = yraw[:, lt % 2, 0:H * w].rearrange("p (h w) -> p h w", h=H)
                    pool.wait_ge(*S.at("rinv_ready", tile + 1))
                    pool.wait_ge(*S.at("yraw_ready", UNITS * k + 4 * lt + 4))
                    if not L.ffn:
                        nv = nully[:, :].rearrange("p (h w) -> p h w", h=H)
                        vn = row[:, R_VN:R_VN + P].rearrange("p (h w) -> p h w", h=H)
                        pool.tensor_tensor(nv, vn, sexp[:, lt % 2, :].unsqueeze(2).broadcast_to(shape), ALU.mult)\
                            .then_inc(S["null_step"], 1)
                        pool.wait_ge(*S.at("null_step", 2 * tile + 1))
                        pool.tensor_tensor(y, y, nv, ALU.add).then_inc(S["null_step"], 1)
                        pool.wait_ge(*S.at("null_step", 2 * tile + 2))
                    pool.tensor_tensor(yn[:, 0:H * w].rearrange("p (h w) -> p h w", h=H), y,
                                       rinv[:, lt % 2, :].unsqueeze(2).broadcast_to(shape), ALU.mult)\
                        .then_inc(S["yn_ready"], 1)

                root(0)
                for n, step in enumerate(L.front):
                    front_step(0, 0, n, *step)

                def body(k, last):
                    for s in range(L.slots):
                        for ahead in (1, 2):
                            if s == L.norm_slot[ahead] and not (last and ahead == 2):
                                root(2 * k + ahead)
                        for place in range(3):
                            misc_steps(L, k, s, last, place, front_step, tail_step)
                        for lt in range(4):
                            if s == 4 * lt + 6:
                                normalise(k, lt)
                            if L.ffn and s == 4 * lt + 9:
                                rms_norm(k, lt)

                rounds(pool, body)

            def experts(number):
                S = moe[number]

                def scale(kk, j):
                    e, s, c = kk * 2 + j // 4, j // 4, j % 4
                    if c == 0:
                        pool.wait_ge(*S.at(f"cb_loaded{s}", (kk + 1) * 16))
                    pool.wait_ge(*S.at("hu_ready", 8 * kk + j + 1))
                    pool.tensor_tensor(he[:, j % 4, :], hu[:, j % 4, :], cb[:, s, 512 * c:512 * c + 512], ALU.mult)\
                        .then_inc(S["h_ready"], 1)

                with pool.Fori(0, E // 2) as kk:
                    for j in range(8):
                        scale(kk, j)

            program(pool, attention, experts)


def kernel(**inputs):
    import concourse.bacc as bacc
    from concourse.bass_utils import run_bass_kernel_spmd

    a = {name.replace("L0_", ""): np.asarray(value) for name, value in inputs.items()}

    def partners(w, group, half):
        n = w.shape[-1]
        parts = w.reshape(w.shape[:-1] + (n // group, 2, group // 2)) if half else \
            w.reshape(w.shape[:-1] + (n // 2, 2, 1))
        return parts[..., ::-1, :].reshape(w.shape)

    qkv, bias = a["ffn_qkv_w"], a["ffn_qkv_b"]
    nqk = (QB + KB) * P
    proj = a["ffn_proj_w"].reshape(QB, P, D).transpose(1, 0, 2).reshape(P, QB * D)
    ffn_w = np.concatenate([qkv[:, :nqk], partners(qkv[:, :nqk], 2, False), qkv[:, nqk:], proj, a["ffn_gate_w"]], axis=1)

    def joint(kind, swap):
        geo = a[f"attn_w{kind}_geo"]
        return np.concatenate([a[f"attn_w{kind}_sem"], partners(geo, HD, True) if swap else geo], axis=1)

    mid_w = np.concatenate([joint("q", False), joint("q", True), joint("k", False), joint("k", True),
                            a["attn_wv"], a["attn_wo"]], axis=1)
    null = np.concatenate([a["attn_k_sem_null"], a["attn_k_geo_null"]])[:, None]
    columns = np.concatenate([bias[:nqk].reshape(-1, P).T, partners(bias[:nqk], 2, False).reshape(-1, P).T,
                              a["ffn_attn_norm_w"][:, None], a["ffn_ffn_norm_w"][:, None], null], axis=1)
    rows = np.concatenate([bias[nqk:], a["ffn_proj_b"], a["ffn_attn_sink"], a["ffn_gate_b"], a["attn_v_null"]])[None, :]
    table, masks = shape_constants()
    host = {"x": a["attn_x"], "table": table, "masks": masks, "ffn_w": ffn_w, "mid_w": mid_w, "columns": columns,
            "rows": rows, "w_up": a["ffn_W_up"], "w_down": a["ffn_W_down"]}

    nc = bacc.Bacc("TRN2", target_bir_lowering=False, num_devices=1)
    arrays, args = {}, {}
    for name, value in host.items():
        value = np.ascontiguousarray(value)
        arrays[f"in_{name}"] = value
        args[name] = nc.dram_tensor(f"in_{name}", value.shape, mybir.dt.from_np(value.dtype), kind="ExternalInput").ap()
    out = nc.dram_tensor("out_x", (BATCH, T, D), F32, kind="ExternalOutput").ap()
    build(nc, out=out, **args)
    result = run_bass_kernel_spmd(nc, [arrays], core_ids=[0])
    return result.results[0]["out_x"]
```

```python
import math
from contextlib import ExitStack

import numpy as np

import concourse.bass as bass
from concourse import mybir

ACT = mybir.ActivationFunctionType
ALU = mybir.AluOpType
AX = mybir.AxisListType
F32 = mybir.dt.float32
F32R = mybir.dt.float32r
BF16 = mybir.dt.bfloat16
U32 = mybir.dt.uint32

BATCH, T, D = 8, 256, 128
P = 128
TILES = BATCH * T // P
TOKENS = BATCH * T
H = 16
G = 4
KV, DH = 4, 64
QB = H * DH // P
KB = KV * DH // P
HD = 4
VD = 8
E, TOPK, DFF = 32, 4, 128
WINDOW = 128
EPS = 1e-5
MASKED = -1e30

ROUNDS = BATCH // 2
UNITS = 2 * 2 * 4
CHUNKS = TOKENS // 512

W_QK, W_SWAP = 0, (QB + KB) * P
W_V = 2 * (QB + KB) * P
W_PROJ = W_V + KV * DH
W_GATE = W_PROJ + QB * D
W_END = W_GATE + E
M_Q, M_QS, M_K, M_KS, M_V, M_O, M_END = (P * i for i in range(7))
C_B, C_BS, C_W1, C_W2, C_NULL, C_END = 0, QB + KB, 2 * (QB + KB), 2 * (QB + KB) + 1, 2 * (QB + KB) + 2, 2 * (QB + KB) + 3
R_BV = 0
R_PB = R_BV + KV * DH
R_SINK = R_PB + D
R_GB = R_SINK + H
R_VN = R_GB + E
R_END = R_VN + P
T_FFN, T_MID = 0, 4 * T
T_ID = 8 * T
T_HEAD = T_ID + P
T_IOTA = T_HEAD + H
T_END = T_IOTA + E
B_ID, B_M0, B_M1, B_END = 0, P, P + 512, P + 1024


def shape_constants():
    f32 = np.float32
    pos = np.arange(T, dtype=f32)

    def rotary(angle, scale, signs):
        return [f32(scale) * np.cos(angle), f32(scale) * np.sin(angle) * signs]

    inv = (f32(1.0) / f32(150000.0) ** (np.arange(0, DH, 2, dtype=f32) / f32(DH))).astype(f32)
    angle = ((pos / f32(32.0))[None, :] * inv[:, None]).astype(f32)
    dim = np.arange(P) % DH
    angle = angle[dim // 2]
    sign = np.where(dim % 2 == 0, -1.0, 1.0).astype(f32)[:, None]
    ffn = rotary(angle, DH ** -0.5, sign) + rotary(angle, 1.0, sign)

    inv = (f32(1.0) / f32(10000.0) ** (np.arange(0, HD, 2, dtype=f32) / f32(HD))).astype(f32)
    angle = (pos[None, :] * inv[:, None]).astype(f32)
    dim = np.arange(P // 2) % HD
    angle = np.concatenate([np.zeros((P // 2, T), f32), angle[dim % (HD // 2)]])
    sign = np.concatenate([np.ones(P // 2), np.where(dim < HD // 2, -1.0, 1.0)]).astype(f32)[:, None]
    mid = rotary(angle, HD ** -0.5, sign) + rotary(angle, 1.0, sign)

    head = (np.arange(P)[:, None] % (P // 2) // HD == np.arange(H)[None, :]).astype(f32)
    iota = np.tile(np.arange(E, dtype=f32), (P, 1))
    table = np.concatenate(ffn + mid + [np.eye(P, dtype=f32), head, iota], axis=1)

    query, key = np.arange(P)[:, None], np.arange(P)[None, :]
    future = np.where(key > query, MASKED, 0.0)
    stale = np.where(P + query - key > WINDOW, MASKED, 0.0)
    masks = [np.eye(P)] + [future] * 4 + [stale, future] * 2
    return np.ascontiguousarray(table, dtype=f32), np.concatenate(masks, axis=1).astype(np.dtype("bfloat16"))



class Signals:

    def __init__(self, sems, past):
        self.sems, self.past = sems, past

    def __getitem__(self, name):
        return self.sems[name]

    def at(self, name, value):
        return self.sems[name], value + self.past[name]


ATTENTION_SIGNALS = dict(
    stats=(2, 2), moments=(2, 2), pow_ready=(2, 1), rstd=(1, 1), xn_ready=(2, 0), normed=(2, 2), xT_ready=(1, 1),
    misc_full=(31, 19), misc_free0=(15.5, 9.5), misc_free1=(15.5, 9.5), cos_ready=(10, 2), q_ready=(8, 1), kT_ready=(0, 1), k_ready=(2, 4),
    v_ready=(2, 2), null_ready=(0, 2), scores_full=(8, 8), rowmax=(8, 8), shift_ready=(8, 8), exp_done=(8, 8),
    pT_full=(8, 8), pT_ready=(8, 8), pT1_ready=(4, 4), yraw_ready=(8, 8), sink_shift=(2, 2),
    sink_exp=(2, 2), denom=(2, 2), rinv_ready=(2, 2), null_step=(0, 4), yn_ready=(2, 2), yT_ready=(4, 2),
    base_ready=(1, 0), x1_ready=(2, 2), square_ready=(2, 0), rms_step=(4, 0), h2_ready=(2, 0), h2T_ready=(2, 0),
    h2_split=(4, 0), gate_step=(10, 0), combine_step=(10, 0), top_shift=(2, 0), top_exp=(2, 0), )
PRIMED = ("combine_step", "exp_done", "pT_ready", "pT1_ready", "yraw_ready", "scores_full", "x1_ready", "h2_split")
EXPERT_SIGNALS = dict(
    combine_out=16, w_loaded0=8 * E, w_loaded1=8 * E, d_loaded0=8 * E, d_loaded1=8 * E,
    d_high=E, d_low=E, h_high=CHUNKS * E, h_low=CHUNKS * E, cb_loaded0=8 * E,
    cb_loaded1=8 * E, w_high=E, w_low=E, ug_full=CHUNKS * E,
    sg_ready=CHUNKS * E, hu_ready=CHUNKS * E, h_ready=CHUNKS * E, down_done=CHUNKS * E, y2T_ready0=2, y2T_ready1=2,
    turn_full=CHUNKS, turned=CHUNKS, cT_full=CHUNKS, cT_ready=CHUNKS)


class Use:

    def __init__(self, n, before):
        self.n, self.before, self.bank = n, before, n % 2

    def number(self, k):
        return self.n + self.before * k if self.before else self.n

    def turn(self, k):
        return self.n // 2 + self.before // 2 * k if self.before else self.n // 2


class Frame:

    def __init__(self, now, steps, weigh):
        self.now, self.steps, self.weigh = now, steps, weigh

    def unit(self, lag):
        for dk, s in self.now:
            if lag <= s < UNITS + lag:
                return dk, s - lag
        return None


class Layer:

    def __init__(self, ffn, signals):
        self.ffn, self.signals = ffn, signals
        self.ropes = QB + KB if ffn else 2
        self.width = DH if ffn else VD
        self.values = KV * DH if ffn else P
        self.lag = lag = 1 if ffn else 2
        self.turns = 2 if ffn else 1
        self.blocks = ["k0", "q0", "q1", "k1"] + [f"q{n}" for n in range(2, QB)] if ffn else ["k0", "q0"]
        rope = [("rope", i) for i in range(self.ropes)]
        value = [("value", 0), ("value", 1)]
        self.front = [("turn_x", 0)] + (rope[:8] + value[:1] + rope[8:] + value[1:] if ffn else
                                        rope + value + [("null", 0), ("null", 1)])
        at = [4, 5, 5, 6, 6, 6, 7, 8, 9, 9, 10, 10, 10] if ffn else [4, 5, 5, 6, 6, 6, 7]
        self.slots = UNITS + (10 if ffn else 7)
        steps = [[] for _ in range(self.slots)]
        for lt in range(4):
            for part in range(self.turns):
                steps[4 * lt + 6 + lag + part].append((0, "turn_y", (lt, part)))
            steps[4 * lt + 8 + lag].append((0, "project", lt))
            if ffn:
                steps[4 * lt + 11].append((0, "turn_h", lt))
                steps[4 * lt + 12].append((0, "gate", lt))
        for ahead in (1, 2):
            for step, slot in zip(self.front, at):
                steps[8 * (ahead - 1) + slot].append((ahead,) + step)
        head = self.slots - UNITS
        self.plan = {}
        n = len(self.front)
        for part in ("start", "loop", "end"):
            frames, n0 = [], n
            for f in range(0, head) if part == "start" else range(head, self.slots):
                now = [(0, f)] + ([(1, f - UNITS)] if part == "loop" and f >= UNITS else [])
                todo = [(dk, step) for dk, s in now for step in steps[s] if not (part == "end" and step[0] == 2)]
                frame = Frame(now, [], None)
                todo.sort(key=lambda what: what[1][0] == 0)
                todo = todo[0:1] + sorted(todo[1:], key=lambda what: what[1][0] != 0)
                order = todo[0:1] + ([None] if frame.unit(lag + 1) else []) + todo[1:]
                for what in order:
                    use = (n, part)
                    n += 1
                    if what is None:
                        frame.weigh = use
                    else:
                        frame.steps.append(what + (use,))
                frames.append(frame)
            self.plan[part] = frames
            if part == "loop":
                per = n - n0
                n = n0 + per * (ROUNDS - 1)
            for frame in frames:
                number = lambda use: Use(use[0], per if part == "loop" else 0)
                frame.steps = [(dk, step, number(use)) for dk, step, use in frame.steps]
                frame.weigh = frame.weigh and number(frame.weigh)
        assert per % 2 == 0 and n == BATCH * ATTENTION_SIGNALS["misc_full"][0 if ffn else 1]


def build(nc, x, table, masks, ffn_w, mid_w, columns, rows, w_up, w_down, out):
    combine_dram = [nc.dram_tensor(f"combine_{n}", (E, TOKENS), F32).ap() for n in range(2)]
    with ExitStack() as ctx:
        def sb(name, shape, dt=F32):
            return ctx.enter_context(nc.sbuf_tensor(name, shape, dt))

        def sem(name):
            return ctx.enter_context(nc.semaphore(name))

        ps = ctx.enter_context(nc.psum_tensor("ps", [P, 8, 512], F32))
        BANK_PT, BANK_MISC = 4, 6
        BANK_U, BANK_G, BANK_ACC = 0, 2, 4

        xr = sb("xr", [P, TILES * D])
        tb = sb("tb", [P, T_END])
        mk = sb("mk", [P, B_END], BF16)
        wf = sb("wf", [P, W_END])
        wm = sb("wm", [P, M_END])
        col = sb("col", [P, C_END])
        row = sb("row", [P, R_END])
        ident = tb[:, T_ID:T_ID + P]
        head_mask = tb[:, T_HEAD:T_HEAD + H]
        iota = tb[:, T_IOTA:T_IOTA + E]
        neg_sink = sb("neg_sink", [P, H])
        null_q = sb("null_q", [P, H])
        bf_zero = sb("bf_zero", [P, 512], BF16)
        stat = sb("stat", [P, 2, 6])
        mv = sb("mv", [P, 2, 2])
        powers = sb("powers", [P, 2, 2])
        rstd = sb("rstd", [P, 2, 2])
        minus_half = sb("minus_half", [P, 4])
        eps = sb("eps", [P, 1])
        xn = sb("xn", [P, 2, D])
        hh = sb("hh", [P, 2, D])
        base = sb("base", [P, 2, 2, D])
        xT = sb("xT", [P, T])
        rot_a = sb("rot_a", [P, 2, T])
        rot_b = sb("rot_b", [P, 2, T])
        qT = sb("qT", [P, 2, QB, T])
        kpad = sb("kpad", [P, 2, KV, 2, T])
        shared = sb("shared", [P, 2 * H * T])
        kz = shared[:, :].rearrange("p (s h t) -> p s h t", s=2, h=H)
        kT = sb("kT", [P, T])
        v = sb("v", [P, 2, 2, KV * DH])
        neg_null = sb("neg_null", [P, 2, 2, H])
        prob = sb("prob", [P, 4, 4, T])
        pT = sb("pT", [P, 2, 2, 512])
        top1 = sb("top1", [P, 2, 4])
        shift = sb("shift", [P, 2, H])
        total = sb("total", [P, 2, H])
        sshift = sb("sshift", [P, 2, H])
        sexp = sb("sexp", [P, 2, H])
        denom = sb("denom", [P, 2, H])
        rinv = sb("rinv", [P, 2, H])
        yraw = sb("yraw", [P, 2, H * DH])
        nully = sb("nully", [P, P])
        yn = sb("yn", [P, H * DH])
        yT = sb("yT", [P, H * DH])
        x1 = sb("x1", [P, D])
        junk = sb("junk", [P, D])
        msq = sb("msq", [P, 1])
        msq_eps = sb("msq_eps", [P, 1])
        rms = sb("rms", [P, 1])
        h2 = sb("h2", [P, D])
        h2T = sb("h2T", [P, P])
        h2h = sb("h2h", [P, TOKENS], F32R)
        h2l = sb("h2l", [P, TOKENS], F32R)
        gl = sb("gl", [P, E])
        top8 = sb("top8", [P, 8])
        idx = sb("idx", [P, 8], U32)
        idxf = sb("idxf", [P, 8])
        ntop = sb("ntop", [P, 1])
        etop = sb("etop", [P, TOPK])
        esum = sb("esum", [P, 1])
        wtop = sb("wtop", [P, TOPK])
        picks = sb("picks", [P, TOPK, E])
        rsum = sb("rsum", [P, 1])
        minus_one = sb("minus_one", [P, 1])
        pairs = sb("pairs", [P, 2, E])
        comb = sb("comb", [P, TILES * E])
        up = sb("up", [P, 2, 2 * DFF])
        uph = sb("uph", [P, 2, 2 * DFF], F32R)
        upl = sb("upl", [P, 2, 2 * DFF], F32R)
        down = sb("down", [P, 2, D])
        dnh = sb("dnh", [P, 2, D], F32R)
        dnl = sb("dnl", [P, 2, D], F32R)
        sg = yraw[:, 0, :].rearrange("p (n t) -> p n t", n=2)
        cb = shared[:, 0:2 * TOKENS].rearrange("p (s t) -> p s t", s=2)
        hu = shared[:, 2 * TOKENS:3 * TOKENS].rearrange("p (n t) -> p n t", n=4)
        he = shared[:, 3 * TOKENS:4 * TOKENS].rearrange("p (n t) -> p n t", n=4)
        cT = shared[0:E, 3 * TOKENS:4 * TOKENS]
        heh = sb("heh", [P, 4, 512], F32R)
        hel = sb("hel", [P, 4, 512], F32R)
        y2T = cb[:, 0, :]

        loaded_first = sem("loaded_first")
        loaded_second = sem("loaded_second")
        loaded_third = sem("loaded_third")
        prep = sem("prep")
        phase_done = sem("phase_done")
        stored = sem("stored")
        mid_sems = {s: sem(f"mid_{s}") for s, n in ATTENTION_SIGNALS.items() if n[1]}
        ffn_sems = {s: sem(f"ffn_{s}") for s, n in ATTENTION_SIGNALS.items() if n[0]}
        expert_sems = {s: sem(f"expert_{s}") for s in EXPERT_SIGNALS}
        layers = [Layer(True, Signals(ffn_sems, {s: int(s in PRIMED) for s in ffn_sems})),
                  Layer(False, Signals(mid_sems, {s: int(s in PRIMED) for s in mid_sems})),
                  Layer(True, Signals(ffn_sems, {s: int(s in PRIMED) + int(BATCH * ATTENTION_SIGNALS[s][0])
                                                 for s in ffn_sems}))]
        moe = [Signals(expert_sems, {s: 0 for s in expert_sems}), Signals(expert_sems, EXPERT_SIGNALS)]
        LOADS = 6, 2, 3
        ENGINES = 5
        PHASES = ("ffn0", "experts0", "mid", "ffn1", "experts1")

        def phase(eng, n):
            eng.drain().then_inc(phase_done, 1)
            eng.wait_ge(phase_done, ENGINES * (n + 1))

        def program(eng, attention, experts):
            attention(layers[0])
            phase(eng, 0)
            experts(0)
            phase(eng, 1)
            attention(layers[1])
            phase(eng, 2)
            attention(layers[2])
            phase(eng, 3)
            experts(1)

        def rounds(eng, body):
            body(0, "start")
            with eng.Fori(0, ROUNDS - 1) as k:
                body(k, "loop")
            body(ROUNDS - 1, "end")

        def take(k, steps, front_step, tail_step):
            for dk, (ahead, kind, arg), use in steps:
                kk = k + dk if dk else k
                bank = ps[:, BANK_MISC + use.bank, :]
                if ahead:
                    front_step(2 * kk + ahead, ahead % 2, bank, use.number(k), use.turn(k), use.bank, kind, arg)
                else:
                    tail_step(kk, bank, use.number(k), use.turn(k), use.bank, kind, arg)

        def first_front(L, front_step):
            for n, (kind, arg) in enumerate(L.front):
                front_step(0, 0, ps[:, BANK_MISC + n % 2, :], n, n // 2, n % 2, kind, arg)

        def at_slot(frame, k, slots):
            for dk, s in frame.now:
                for n, slot in enumerate(slots):
                    if s == slot:
                        yield (k + dk if dk else k), n

        def ahead_at(frame, k, part, slot):
            for dk, s in frame.now:
                for ahead in (1, 2):
                    if s == 8 * (ahead - 1) + slot and not (part == "end" and ahead == 2):
                        yield 2 * (k + dk if dk else k) + ahead, ahead % 2

        def block_of(L, i):
            return int(L.blocks[i][1:]) + (QB if L.blocks[i][0] == "k" else 0)

        def queries_by(L, i):
            return sum(name[0] == "q" for name in L.blocks[:i + 1])

        def later(b):
            return not (isinstance(b, int) and b == 0)

        def keys(lt):
            return P * (lt % 2 + 1)

        def score_view(n, lt):
            if lt % 2 == 0:
                return ps[:, 2 * (n % 2), :].rearrange("p (h k) -> p h k", h=4)
            return ps[:, 2 * (n % 2):2 * (n % 2) + 2, :].rearrange("p b (h k) -> p (b h) k", h=2)

        block = ctx.enter_context(nc.Block())

        @block.sync
        def _(sp):
            tokens = x.rearrange("b (t p) d -> p (b t) d", p=P)
            stream = xr[:, :].rearrange("p (c d) -> p c d", d=D)

            def load(to, source, group):
                sp.dma_start(to, source).then_inc(group, 16)

            load(stream[:, 0:4, :], tokens[:, 0:4, :], loaded_first)
            load(tb[:, T_ID:T_END], table[:, T_ID:T_END], loaded_first)
            load(col[:, :], columns, loaded_first)
            load(row[:, :], rows.broadcast_to([P, R_END]), loaded_first)
            load(wf[:, 0:W_V], ffn_w[:, 0:W_V], loaded_first)
            load(tb[:, T_FFN:T_MID], table[:, T_FFN:T_MID], loaded_first)
            load(wf[:, W_V:W_END], ffn_w[:, W_V:W_END], loaded_second)
            load(mk[:, :], masks, loaded_second)
            load(stream[:, 4:TILES, :], tokens[:, 4:TILES, :], loaded_third)
            load(tb[:, T_MID:T_ID], table[:, T_MID:T_ID], loaded_third)
            load(wm[:, :], mid_w, loaded_third)

            def load_up(S, e, s):
                sp.dma_start(up[:, s, :], w_up[bass.ds(e, 1), :, :].rearrange("e d f -> d (e f)"))\
                    .then_inc(S[f"w_loaded{s}"], 16)

            def load_down(S, e, s):
                sp.dma_start(down[:, s, :], w_down[bass.ds(e, 1), :, :].rearrange("e f d -> f (e d)"))\
                    .then_inc(S[f"d_loaded{s}"], 16)

            def attention(L):
                if L.ffn:
                    for e in range(2):
                        load_up(moe[layers.index(L) // 2], e, e)
                        load_down(moe[layers.index(L) // 2], e, e)

            def experts(number):
                S = moe[number]
                dram = combine_dram[number]
                sp.wait_ge(*S.at("cT_ready", CHUNKS))
                sp.dma_start(dram, cT[:, :]).then_inc(S["combine_out"], 16)
                sp.wait_ge(*S.at("combine_out", 16))

                def load_weight(e, s):
                    sp.dma_start(cb[:, s, :], dram[bass.ds(e, 1), :].broadcast_to([P, TOKENS]))\
                        .then_inc(S[f"cb_loaded{s}"], 16)

                def load(e, s):
                    sp.wait_ge(*S.at("w_low", e - 1))
                    sp.wait_ge(*S.at("combine_out", 16))
                    load_up(S, e, s)
                    sp.wait_ge(*S.at("h_ready", CHUNKS * (e - 1)))
                    sp.wait_ge(*S.at("combine_out", 16))
                    load_weight(e, s)
                    sp.wait_ge(*S.at("d_low", e - 1))
                    sp.wait_ge(*S.at("combine_out", 16))
                    load_down(S, e, s)

                load_weight(0, 0)
                load_weight(1, 1)
                with sp.Fori(1, E // 2) as kk:
                    for s in range(2):
                        load(kk * 2 + s, s)

            program(sp, attention, experts)
            sp.wait_ge(*moe[1].at("turned", CHUNKS))
            sp.dma_start(out.rearrange("b (t p) d -> p (b t) d", p=P),
                         xr[:, :].rearrange("p (c d) -> p c d", d=D)).then_inc(stored, 16)
            sp.wait_ge(stored, 16)

        @block.tensor
        def _(pe):
            pe.wait_ge(loaded_first, 16 * LOADS[0])
            pe.wait_ge(prep, 6)

            def attention(L):
                S = L.signals

                def front_step(b, par, misc, use, turn, bank, kind, i):
                    pe.wait_ge(*S.at(f"misc_free{bank}", turn))
                    if kind == "turn_x":
                        pe.wait_ge(*S.at("normed", 2 * b + 2))
                        for t in range(2):
                            last = pe.transpose(misc[:, t * P:(t + 1) * P], (hh if L.ffn else xn)[:, t, :], ident)
                    elif kind == "rope":
                        pe.wait_ge(*S.at("xT_ready", b + 1))
                        if L.ffn:
                            blk = block_of(L, i)
                            pair = wf[:, W_QK + blk * P:], wf[:, W_SWAP + blk * P:]
                        else:
                            pair = ((wm[:, M_K:], wm[:, M_KS:]), (wm[:, M_Q:], wm[:, M_QS:]))[i]
                        for n, w in enumerate(pair):
                            last = pe.matmul(misc[:, n * T:(n + 1) * T], w[:, 0:P], xT[:, :], start=True, stop=True)
                    elif kind == "value":
                        if not later(b) and L is layers[0]:
                            pe.wait_ge(loaded_second, 16 * LOADS[1])
                        w = wf[:, W_V:W_V + KV * DH] if L.ffn else wm[:, M_V:M_V + P]
                        last = pe.matmul(misc[:, 0:L.values], xT[:, i * P:(i + 1) * P], w, start=True, stop=True)
                    elif kind == "null":
                        pe.wait_ge(*S.at("q_ready", b + 1))
                        last = pe.matmul(misc[:, 0:H], qT[:, par, 0, i * P:(i + 1) * P], null_q[:, :],
                                         start=True, stop=True)
                    last.then_inc(S["misc_full"], 1)

                def tail_step(k, misc, use, turn, bank, kind, arg):
                    lt = arg[0] if kind == "turn_y" else arg
                    tile = 4 * k + lt
                    pe.wait_ge(*S.at(f"misc_free{bank}", turn))
                    if kind == "turn_y":
                        pe.wait_ge(*S.at("yn_ready", tile + 1))
                        blocks = 4 if L.ffn else 1
                        for n in range(blocks):
                            c = (arg[1] * blocks + n) * P
                            last = pe.transpose(misc[:, n * P:(n + 1) * P], yn[:, c:c + P], ident)
                    elif kind == "project":
                        pe.wait_ge(*S.at("yT_ready", L.turns * (tile + 1)))
                        blocks = QB if L.ffn else 1
                        for n in range(blocks):
                            w = wf[:, W_PROJ + n * D:W_PROJ + (n + 1) * D] if L.ffn else wm[:, M_O:M_O + D]
                            last = pe.matmul(misc[:, 0:D], yT[:, n * P:(n + 1) * P], w,
                                             start=(n == 0), stop=(n == blocks - 1))
                    elif kind == "turn_h":
                        pe.wait_ge(*S.at("h2_ready", tile + 1))
                        last = pe.transpose(misc[:, 0:P], h2[:, :], ident)
                    elif kind == "gate":
                        pe.wait_ge(*S.at("h2T_ready", tile + 1))
                        last = pe.matmul(misc[:, 0:E], h2T[:, :], wf[:, W_GATE:W_GATE + E], start=True, stop=True)
                    last.then_inc(S["misc_full"], 1)

                def scores(k, s, half):
                    b, j, lt, g = 2 * k + s // 8, s // 8, s // 4, s % 4
                    if half == 0 and (later(k) or s > 1):
                        pe.wait_ge(*S.at("exp_done", UNITS * k + s - 1))
                    if half == 0 and L.ffn:
                        pe.wait_ge(*S.at("q_ready", QB * b + 2 * g + 2))
                        pe.wait_ge(*S.at("k_ready", KB * b + g // 2 + 1))
                    elif half == 0:
                        pe.wait_ge(*S.at("q_ready", b + 1))
                        pe.wait_ge(*S.at("k_ready", G * b + g + 1))
                    bank = 2 * (s % 2)
                    q0 = (lt % 2) * P
                    n = half
                    blk = 2 * g + n if L.ffn else 0
                    q = qT[:, j, blk, q0:q0 + P]
                    heads = kpad[:, j, g, :, 0:keys(lt)] if L.ffn else \
                        kz[:, j, 4 * g + 2 * n:4 * g + 2 * n + 2, 0:keys(lt)]
                    if lt % 2 == 0:
                        if n == 0:
                            pe.matmul(ps[:, bank, :], mk[:, B_ID:B_ID + P], mk[:, B_M0:B_M0 + 512],
                                      start=True, stop=False)
                        to = ps[:, bank, 256 * n:256 * n + 256]
                    else:
                        if L.ffn:
                            pe.matmul(ps[:, bank + n, :], mk[:, B_ID:B_ID + P], mk[:, B_M1:B_M1 + 512],
                                      start=True, stop=False)
                        to = ps[:, bank + n, :]
                    to = to.rearrange("p (h k) -> p h k", h=2)
                    behind = not L.ffn and lt % 2 == 1
                    last = pe.matmul(to, q, heads, start=behind, stop=not behind and (lt % 2 == 1 or n == 1))
                    if behind:
                        last = pe.matmul(to[:, :, P:T], mk[:, B_ID:B_ID + P],
                                         mk[:, B_M0:B_M0 + 2 * P].rearrange("p (h k) -> p h k", h=2),
                                         start=False, stop=True)
                    if half:
                        last.then_inc(S["scores_full"], 1)

                def turn_probs(k, s):
                    lt = s // 4
                    pe.wait_ge(*S.at("exp_done", UNITS * k + s + 1))
                    pe.wait_ge(*S.at("pT_ready", UNITS * k + s))
                    if lt > 0:
                        pe.wait_ge(*S.at("pT1_ready", UNITS // 2 * k + 4 * (lt // 2) + (s % 4 if lt % 2 else 0)))
                    for c in range(keys(lt) // P):
                        for h in range(4):
                            last = pe.transpose(ps[:, BANK_PT + c, h * P:(h + 1) * P],
                                                prob[:, s % 4, h, c * P:(c + 1) * P], ident)
                    last.then_inc(S["pT_full"], 1)

                def weigh(k, s, y, turn, bank):
                    pe.wait_ge(*S.at(f"misc_free{bank}", turn))
                    b, j, lt, g = 2 * k + s // 8, s // 8, s // 4, s % 4
                    pe.wait_ge(*S.at("pT_ready", UNITS * k + s + 1))
                    if lt % 2:
                        pe.wait_ge(*S.at("pT1_ready", G * b + g + 1))
                    pe.wait_ge(*S.at("v_ready", 2 * b + 1 + lt % 2))
                    w = L.width
                    for h in range(4):
                        for c in range(keys(lt) // P):
                            at = g * DH if L.ffn else (4 * g + h) * VD
                            last = pe.matmul(y[:, h * w:(h + 1) * w], pT[:, s % 2, c, h * P:(h + 1) * P],
                                             v[:, j, c, at:at + w], start=(c == 0), stop=(c == lt % 2))
                    last.then_inc(S["misc_full"], 1)

                first_front(L, front_step)

                def body(k, part):
                    for frame in L.plan[part]:
                        if frame.unit(0):
                            dk, s = frame.unit(0)
                            scores(k + dk if dk else k, s, 0)
                        take(k, frame.steps[0:1], front_step, tail_step)
                        if frame.unit(0):
                            scores(k + dk if dk else k, s, 1)
                        if frame.unit(L.lag + 1):
                            dk, s = frame.unit(L.lag + 1)
                            use = frame.weigh
                            weigh(k + dk if dk else k, s, ps[:, BANK_MISC + use.bank, :], use.turn(k), use.bank)
                        if frame.unit(L.lag):
                            dk, s = frame.unit(L.lag)
                            turn_probs(k + dk if dk else k, s)
                        take(k, frame.steps[1:], front_step, tail_step)

                rounds(pe, body)

            def experts(number):
                S = moe[number]
                zero = bf_zero
                for n in range(TILES):
                    last = pe.transpose(ps[0:E, n // 4, n % 4 * P:(n % 4 + 1) * P], comb[:, n * E:(n + 1) * E], ident)
                    if n % 4 == 3:
                        last.then_inc(S["cT_full"], 1)
                for c in range(CHUNKS):
                    last = pe.matmul(ps[:, BANK_ACC + c, :], zero[:, 0:P], zero[:, :], start=True, stop=False,
                                     skip_group_check=True)

                def ups(kk, j, wait):
                    e, s, c, two = kk * 2 + j // 4, j // 4 % 2, j % 4, j % 2
                    if c == 0:
                        pe.wait_ge(*S.at("w_low", e + 1))
                    if wait:
                        pe.wait_ge(*S.at("hu_ready", 8 * kk + j - 1))
                    xs = slice(512 * c, 512 * c + 512)
                    for n, bank in enumerate((BANK_U, BANK_G)):
                        f = slice(n * DFF, (n + 1) * DFF)
                        to = ps[:, bank + two, :]
                        pe.matmul(to, uph[:, s, f], h2h[:, xs], start=True, stop=False)
                        pe.matmul(to, uph[:, s, f], h2l[:, xs], start=False, stop=False)
                        last = pe.matmul(to, upl[:, s, f], h2h[:, xs], start=False, stop=True)
                    last.then_inc(S["ug_full"], 1)

                def downs(kk, j, final):
                    e, s, c = kk * 2 + j // 4, j // 4, j % 4
                    if c == 0:
                        pe.wait_ge(*S.at("d_low", e + 1))
                    pe.wait_ge(*S.at("h_low", 8 * kk + j + 1))
                    to = ps[:, BANK_ACC + c, :]
                    pe.matmul(to, dnh[:, s, :], heh[:, j % 4, :], start=False, stop=False, skip_group_check=True)
                    pe.matmul(to, dnl[:, s, :], heh[:, j % 4, :], start=False, stop=False, skip_group_check=True)
                    pe.matmul(to, dnh[:, s, :], hel[:, j % 4, :], start=False, stop=final,
                              skip_group_check=True).then_inc(S["down_done"], 1)

                pe.wait_ge(*S.at("cT_ready", CHUNKS))
                ups(0, 0, False)
                ups(0, 1, False)
                ups(0, 2, True)

                def body(kk, last):
                    for j in range(8):
                        if not (last and j >= 5):
                            ups(kk, j + 3, True)
                        downs(kk, j, last and j >= 4)

                with pe.Fori(0, E // 2 - 1) as kk:
                    body(kk, False)
                body(E // 2 - 1, True)
                for n in range(TILES):
                    pe.wait_ge(*S.at(f"y2T_ready{n // 4 % 2}", n // 8 + 1))
                    last = pe.transpose(ps[:, n // 4, n % 4 * P:(n % 4 + 1) * P], y2T[:, n * P:(n + 1) * P], ident)
                    if n % 4 == 3:
                        last.then_inc(S["turn_full"], 1)

            program(pe, attention, experts)

        @block.vector
        def _(dve):
            for sems in (ffn_sems, mid_sems):
                for name in PRIMED:
                    if name in sems:
                        dve.sem_inc(sems[name], 1)
            dve.memset(kpad[:, :, :, :, :], 0.0).then_inc(prep, 1)
            dve.memset(bf_zero[:, :], 0.0).then_inc(prep, 1)
            dve.wait_ge(loaded_first, 16 * LOADS[0])
            dve.tensor_scalar(neg_sink[:, :], row[:, R_SINK:R_SINK + H], -1.0, None, ALU.mult).then_inc(prep, 1)
            dve.tensor_scalar(null_q[:, :], head_mask, col[:, C_NULL:C_NULL + 1], None, ALU.mult).then_inc(prep, 1)
            dve.memset(eps[:, :], EPS).then_inc(prep, 1)
            dve.memset(minus_one[:, :], -1.0)
            dve.memset(minus_half[:, :], -0.5).then_inc(prep, 1)
            dve.wait_ge(prep, 6)

            def attention(L):
                S = L.signals

                def statistics(b):
                    for t in range(2):
                        xt = xr[:, bass.ds(b * T + t * P, P)]
                        dve.bn_stats(stat[:, t, :], xt).then_inc(S["stats"], 1)

                def moments(b):
                    for t in range(2):
                        dve.bn_aggr(mv[:, t, :], stat[:, t, :]).then_inc(S["moments"], 1)
                    dve.wait_ge(*S.at("moments", 2 * b + 2))
                    dve.tensor_scalar(powers[:, 0, :], mv[:, :, 1], EPS, None, ALU.add).then_inc(S["pow_ready"], 1)
                    if L.ffn:
                        dve.tensor_scalar(powers[:, 1, :], mv[:, :, 1], 1.0 + EPS, EPS * EPS, ALU.mult, ALU.add)\
                            .then_inc(S["pow_ready"], 1)

                def norm(b):
                    dve.wait_ge(*S.at("rstd", b + 1))
                    if later(b):
                        dve.wait_ge(*S.at("xT_ready", b))
                        if L.ffn:
                            dve.wait_ge(*S.at("base_ready", b))
                    for t in range(2):
                        xt = xr[:, bass.ds(b * T + t * P, P)]
                        dve.tensor_scalar(xn[:, t, :], xt, mv[:, t, 0:1], rstd[:, 0, t:t + 1], ALU.subtract,
                                          ALU.mult).then_inc(S["xn_ready" if L.ffn else "normed"], 1)
                    if L.ffn:
                        for t in range(2):
                            xt = xr[:, bass.ds(b * T + t * P, P)]
                            dve.tensor_scalar(hh[:, t, :], xt, mv[:, t, 0:1], rstd[:, 1, t:t + 1], ALU.subtract,
                                              ALU.mult).then_inc(S["normed"], 1)

                def front_step(b, par, misc, use, turn, bank, kind, i):
                    if kind == "rope":
                        if L.ffn:
                            if i < 2:
                                if later(b):
                                    dve.wait_ge(*S.at("q_ready", QB * b))
                            elif L.blocks[i - 2][0] == "q":
                                dve.wait_ge(*S.at("q_ready", QB * b + queries_by(L, i - 2)))
                            else:
                                dve.wait_ge(*S.at("k_ready", KB * b + i - 1 - queries_by(L, i - 2)))
                        else:
                            dve.wait_ge(*S.at("q_ready" if i else "kT_ready", b))
                        dve.wait_ge(*S.at("misc_full", use + 1))
                        is_key = L.blocks[i][0] == "k"
                        t0 = (T_FFN if L.ffn else T_MID) + (2 * T if is_key else 0)
                        for n, to in enumerate((rot_a, rot_b)):
                            src, angle = misc[:, n * T:(n + 1) * T], tb[:, t0 + n * T:t0 + (n + 1) * T]
                            if L.ffn:
                                blk = block_of(L, i)
                                bias = col[:, C_B + blk:C_B + blk + 1] if n == 0 else \
                                    col[:, C_BS + blk:C_BS + blk + 1]
                                last = dve.scalar_tensor_tensor(to[:, i % 2, :], src, bias, angle, ALU.add, ALU.mult)
                            else:
                                last = dve.tensor_tensor(to[:, i, :], src, angle, ALU.mult)
                            last.then_inc(S[f"misc_free{bank}" if n else "cos_ready"], 1)
                        if L.ffn and is_key:
                            dve.wait_ge(*S.at("cos_ready", L.ropes * b + i + 1))
                            dve.wait_ge(*S.at(f"misc_free{bank}", turn + 1))
                            dve.wait_ge(*S.at("scores_full", 8 * (b - 1) if later(b) else 0))
                            kb = int(L.blocks[i][1:])
                            for half in range(2):
                                src = slice(64 * half, 64 * half + 64)
                                for place in range(2):
                                    dst = slice(64 * place, 64 * place + 64)
                                    last = dve.tensor_tensor(kpad[dst, par, 2 * kb + half, place, :],
                                                             rot_a[src, i % 2, :], rot_b[src, i % 2, :], ALU.add)
                            last.then_inc(S["k_ready"], 1)
                    elif kind == "value":
                        dve.wait_ge(*S.at("misc_full", use + 1))
                        if later(b):
                            dve.wait_ge(*S.at("yraw_ready", 8 * (b - 1)))
                        if L.ffn:
                            dve.tensor_tensor(v[:, par, i, :], misc[:, 0:KV * DH], row[:, R_BV:R_BV + KV * DH],
                                              ALU.add).then_inc(S["v_ready"], 1)
                        else:
                            dve.tensor_copy(v[:, par, i, 0:P], misc[:, 0:P]).then_inc(S["v_ready"], 1)
                        dve.wait_ge(*S.at("v_ready", 2 * b + i + 1))
                        dve.sem_inc(S[f"misc_free{bank}"], 1)
                    elif kind == "null":
                        dve.wait_ge(*S.at("misc_full", use + 1))
                        dve.tensor_scalar(neg_null[:, par, i, :], misc[:, 0:H], -1.0, None, ALU.mult)\
                            .then_inc(S["null_ready"], 1)
                        dve.wait_ge(*S.at("null_ready", 2 * b + i + 1))
                        dve.sem_inc(S[f"misc_free{bank}"], 1)

                def negated(lt):
                    return neg_sink[:, :] if L.ffn else neg_null[:, lt // 2, lt % 2, :]

                def row_max(k, s):
                    lt, g = s // 4, s % 4
                    dve.wait_ge(*S.at("scores_full", UNITS * k + s + 1))
                    dve.tensor_reduce(top1[:, s % 2, :], score_view(s, lt), AX.X, ALU.max, negate=True)\
                        .then_inc(S["rowmax"], 1)
                    dve.wait_ge(*S.at("rowmax", UNITS * k + s + 1))
                    dve.tensor_tensor(shift[:, lt % 2, 4 * g:4 * g + 4], top1[:, s % 2, :],
                                      negated(lt)[:, 4 * g:4 * g + 4], ALU.min).then_inc(S["shift_ready"], 1)

                def copy_pT(k, s):
                    dve.wait_ge(*S.at("pT_full", UNITS * k + s + 1))
                    dve.tensor_copy(pT[:, s % 2, 0, :], ps[:, BANK_PT, :]).then_inc(S["pT_ready"], 1)

                def sink_shift(k, lt):
                    dve.wait_ge(*S.at("shift_ready", UNITS * k + 4 * lt + 4))
                    dve.tensor_tensor(sshift[:, lt % 2, :], shift[:, lt % 2, :], negated(lt), ALU.subtract)\
                        .then_inc(S["sink_shift"], 1)

                def normaliser(k, lt):
                    tile = 4 * k + lt
                    dve.wait_ge(*S.at("exp_done", UNITS * k + 4 * lt + 4))
                    dve.wait_ge(*S.at("sink_exp", tile + 1))
                    dve.tensor_tensor(denom[:, lt % 2, :], total[:, lt % 2, :], sexp[:, lt % 2, :], ALU.add)\
                        .then_inc(S["denom"], 1)
                    dve.wait_ge(*S.at("denom", tile + 1))
                    dve.reciprocal(rinv[:, lt % 2, :], denom[:, lt % 2, :]).then_inc(S["rinv_ready"], 1)

                def tail_step(k, misc, use, turn, bank, kind, arg):
                    if kind not in ("project", "gate"):
                        return
                    lt = arg
                    tile = 4 * k + lt
                    xt = xr[:, bass.ds(tile * P, P)]
                    dve.wait_ge(*S.at("misc_full", use + 1))
                    if kind == "project" and L.ffn:
                        dve.tensor_tensor(x1[:, :], misc[:, 0:D], base[:, lt // 2, lt % 2, :], ALU.add)\
                            .then_inc(S["x1_ready"], 1)
                        dve.wait_ge(*S.at("x1_ready", tile + 1))
                        dve.sem_inc(S[f"misc_free{bank}"], 1)
                        dve.scalar_tensor_tensor(xt, x1[:, :], 0.5, xt, ALU.mult, ALU.add)
                    elif kind == "project":
                        dve.tensor_tensor(xt, misc[:, 0:D], xt, ALU.add).then_inc(S["x1_ready"], 1)
                        dve.wait_ge(*S.at("x1_ready", tile + 1))
                        dve.sem_inc(S[f"misc_free{bank}"], 1)
                    elif kind == "gate":
                        G0 = 5 * tile
                        dve.wait_ge(*S.at("combine_step", 5 * tile))
                        dve.tensor_tensor(gl[:, :], misc[:, 0:E], row[:, R_GB:R_GB + E], ALU.add)\
                            .then_inc(S["gate_step"], 1)
                        dve.wait_ge(*S.at("gate_step", G0 + 1))
                        dve.sem_inc(S[f"misc_free{bank}"], 1)
                        dve.max(out=top8[:, :], in_=gl[:, :]).then_inc(S["gate_step"], 1)
                        dve.wait_ge(*S.at("gate_step", G0 + 2))
                        dve.tensor_scalar(ntop[:, :], top8[:, 0:1], -1.0, None, ALU.mult).then_inc(S["top_shift"], 1)
                        dve.max_index(out=idx[:, :], in_max=top8[:, :], in_values=gl[:, :])\
                            .then_inc(S["gate_step"], 1)
                        dve.wait_ge(*S.at("gate_step", G0 + 3))
                        dve.tensor_copy(idxf[:, :], idx[:, :]).then_inc(S["gate_step"], 1)
                        dve.wait_ge(*S.at("gate_step", G0 + 4))
                        shape = [P, TOPK, E]
                        dve.tensor_tensor(picks[:, :, :], iota.unsqueeze(1).broadcast_to(shape),
                                          idxf[:, 0:TOPK].unsqueeze(2).broadcast_to(shape), ALU.is_equal)\
                            .then_inc(S["gate_step"], 1)

                def split_h2(k, lt):
                    tile = 4 * k + lt
                    high, low = h2h[:, bass.ds(tile * P, P)], h2l[:, bass.ds(tile * P, P)]
                    dve.wait_ge(*S.at("h2T_ready", tile + 1))
                    dve.tensor_copy(high, h2T[:, :]).then_inc(S["h2_split"], 1)
                    dve.wait_ge(*S.at("h2_split", 2 * tile + 1))
                    dve.tensor_tensor(low, h2T[:, :], high.bitcast(F32), ALU.subtract).then_inc(S["h2_split"], 1)

                statistics(0)
                dve.wait_ge(*S.at("stats", 2))
                moments(0)
                norm(0)
                first_front(L, front_step)
                if L is layers[0]:
                    dve.wait_ge(loaded_third, 16 * LOADS[2])

                def body(k, part):
                    for frame in L.plan[part]:
                        take(k, frame.steps[0:1], front_step, tail_step)
                        if frame.unit(0):
                            dk, s = frame.unit(0)
                            row_max(k + dk if dk else k, s)
                        for kk, lt in at_slot(frame, k, (4, 8, 12, 16)):
                            sink_shift(kk, lt)
                        for b, par in ahead_at(frame, k, part, 3):
                            moments(b)
                        if frame.unit(L.lag):
                            dk, s = frame.unit(L.lag)
                            copy_pT(k + dk if dk else k, s)
                        take(k, frame.steps[1:], front_step, tail_step)
                        for b, par in ahead_at(frame, k, part, 3):
                            norm(b)
                        for kk, lt in at_slot(frame, k, (5, 9, 13, 17)):
                            normaliser(kk, lt)
                        if L.ffn:
                            for kk, lt in at_slot(frame, k, (12, 16, 20, 24)):
                                split_h2(kk, lt)
                        for b, par in ahead_at(frame, k, part, 2):
                            statistics(b)
                            dve.wait_ge(*S.at("stats", 2 * b + 2))

                rounds(dve, body)

            def experts(number):
                S = moe[number]

                def split(kk, s, wait):
                    dve.wait_ge(*S.at(f"w_loaded{s}", (kk + 1) * 16))
                    if wait:
                        dve.wait_ge(*S.at("ug_full", CHUNKS * (kk * 2 + s - 1)))
                    dve.tensor_copy(uph[:, s, :], up[:, s, :]).then_inc(S["w_high"], 1)
                    dve.wait_ge(*S.at("w_high", kk * 2 + s + 1))
                    dve.tensor_tensor(upl[:, s, :], up[:, s, :], uph[:, s, :].bitcast(F32), ALU.subtract)\
                        .then_inc(S["w_low"], 1)

                def split_down(kk, s, wait):
                    dve.wait_ge(*S.at(f"d_loaded{s}", (kk + 1) * 16))
                    if wait:
                        dve.wait_ge(*S.at("ug_full", CHUNKS * (kk * 2 + s)))
                    dve.tensor_copy(dnh[:, s, :], down[:, s, :]).then_inc(S["d_high"], 1)
                    dve.wait_ge(*S.at("d_high", kk * 2 + s + 1))
                    dve.tensor_tensor(dnl[:, s, :], down[:, s, :], dnh[:, s, :].bitcast(F32), ALU.subtract)\
                        .then_inc(S["d_low"], 1)

                def low_part(kk, j):
                    dve.wait_ge(*S.at("h_high", 8 * kk + j + 1))
                    dve.tensor_tensor(hel[:, j % 4, :], he[:, j % 4, :], heh[:, j % 4, :].bitcast(F32), ALU.subtract)\
                        .then_inc(S["h_low"], 1)

                def gated(kk, j):
                    dve.wait_ge(*S.at("sg_ready", 8 * kk + j + 1))
                    dve.tensor_tensor(hu[:, j % 4, :], ps[:, BANK_U + j % 2, :], sg[:, j % 2, :], ALU.mult)\
                        .then_inc(S["hu_ready"], 1)

                split(0, 0, False)
                split(0, 1, False)
                split_down(0, 0, False)
                gated(0, 0)

                def body(kk, last):
                    for j in range(8):
                        if not (last and j == 7):
                            gated(kk, j + 1)
                        low_part(kk, j)
                        if j == 2:
                            if not last:
                                split(kk + 1, 0, True)
                            split_down(kk, 1, True)
                        if j == 6 and not last:
                            split(kk + 1, 1, True)
                            split_down(kk + 1, 0, True)

                with dve.Fori(0, E // 2 - 1) as kk:
                    body(kk, False)
                body(E // 2 - 1, True)
                for c in (0, 2):
                    dve.wait_ge(*S.at("down_done", CHUNKS * (E - 1) + c + 1))
                    dve.tensor_copy(y2T[:, 512 * c:512 * c + 512], ps[:, BANK_ACC + c, :]).then_inc(S["y2T_ready0"], 1)
                for c in range(CHUNKS):
                    xt = xr[:, 512 * c:512 * c + 512]
                    dve.wait_ge(*S.at("turn_full", c + 1))
                    dve.scalar_tensor_tensor(xt, ps[:, c, :], 0.5, xt, ALU.mult, ALU.add).then_inc(S["turned"], 1)

            program(dve, attention, experts)

        @block.scalar
        def _(act):
            act.wait_ge(loaded_first, 16 * LOADS[0])
            act.wait_ge(prep, 6)

            def attention(L):
                S = L.signals

                def release(copied, value, bank):
                    act.wait_ge(*S.at(copied, value))
                    act.sem_inc(S[f"misc_free{bank}"], 1)

                def front_step(b, par, misc, use, turn, bank, kind, i):
                    if kind == "turn_x":
                        act.wait_ge(*S.at("misc_full", use + 1))
                        if L.ffn:
                            act.activation(xT[:, :], misc[:, 0:T], ACT.Copy, scale=col[:, C_W1:C_W1 + 1])\
                                .then_inc(S["xT_ready"], 1)
                        else:
                            act.activation(xT[:, :], misc[:, 0:T], ACT.Copy).then_inc(S["xT_ready"], 1)
                        release("xT_ready", b + 1, bank)

                def exps(k, s):
                    lt, g = s // 4, s % 4
                    act.wait_ge(*S.at("shift_ready", UNITS * k + s + 1))
                    for h in range(4):
                        one = 4 * g + h
                        last = act.activation(prob[:, s % 4, h, 0:keys(lt)], score_view(s, lt)[:, h, :], ACT.Exp,
                                              bias=shift[:, lt % 2, one:one + 1],
                                              accum_out=total[:, lt % 2, one:one + 1])
                    last.then_inc(S["exp_done"], 1)

                def sink_exp(k, lt):
                    act.wait_ge(*S.at("sink_shift", 4 * k + lt + 1))
                    act.activation(sexp[:, lt % 2, :], sshift[:, lt % 2, :], ACT.Exp).then_inc(S["sink_exp"], 1)

                def copy_pT1(k, s):
                    act.wait_ge(*S.at("pT_full", UNITS * k + s + 1))
                    act.activation(pT[:, s % 2, 1, :], ps[:, BANK_PT + 1, :], ACT.Copy).then_inc(S["pT1_ready"], 1)

                def copy_y(k, s, y, use, bank):
                    lt, g = s // 4, s % 4
                    act.wait_ge(*S.at("misc_full", use + 1))
                    n = 4 * L.width
                    act.activation(yraw[:, lt % 2, g * n:(g + 1) * n], y[:, 0:n], ACT.Copy)\
                        .then_inc(S["yraw_ready"], 1)
                    release("yraw_ready", UNITS * k + s + 1, bank)

                def tail_step(k, misc, use, turn, bank, kind, arg):
                    lt = arg[0] if kind == "turn_y" else arg
                    tile = 4 * k + lt
                    if kind == "turn_y":
                        n = 4 * P if L.ffn else P
                        act.wait_ge(*S.at("misc_full", use + 1))
                        act.activation(yT[:, arg[1] * n:(arg[1] + 1) * n], misc[:, 0:n], ACT.Copy)\
                            .then_inc(S["yT_ready"], 1)
                        release("yT_ready", L.turns * tile + arg[1] + 1, bank)
                    elif kind == "project" and L.ffn:
                        act.wait_ge(*S.at("x1_ready", tile + 1))
                        act.activation(junk[:, :], x1[:, :], ACT.Square, scale=D ** -0.5, accum_out=msq[:, :])\
                            .then_inc(S["square_ready"], 1)
                    elif kind == "turn_h":
                        act.wait_ge(*S.at("misc_full", use + 1))
                        act.wait_ge(*S.at("h2_split", 2 * tile))
                        act.activation(h2T[:, :], misc[:, 0:P], ACT.Copy, scale=col[:, C_W2:C_W2 + 1])\
                            .then_inc(S["h2T_ready"], 1)
                        release("h2T_ready", tile + 1, bank)
                    elif kind == "gate":
                        act.wait_ge(*S.at("top_shift", tile + 1))
                        act.activation(etop[:, :], top8[:, 0:TOPK], ACT.Exp, bias=ntop[:, :], accum_out=esum[:, :])\
                            .then_inc(S["top_exp"], 1)

                first_front(L, front_step)

                def body(k, part):
                    for frame in L.plan[part]:
                        take(k, frame.steps[0:1], front_step, tail_step)
                        if frame.unit(L.lag + 1):
                            dk, s = frame.unit(L.lag + 1)
                            use = frame.weigh
                            copy_y(k + dk if dk else k, s, ps[:, BANK_MISC + use.bank, :], use.number(k), use.bank)
                        copies = frame.unit(L.lag) and frame.unit(L.lag)[1] // 4 % 2
                        if copies and L.lag > 1:
                            dk, s = frame.unit(L.lag)
                            copy_pT1(k + dk if dk else k, s)
                        if frame.unit(0):
                            dk, s = frame.unit(0)
                            exps(k + dk if dk else k, s)
                        for kk, lt in at_slot(frame, k, (4, 8, 12, 16)):
                            sink_exp(kk, lt)
                        if copies and L.lag == 1:
                            dk, s = frame.unit(L.lag)
                            copy_pT1(k + dk if dk else k, s)
                        take(k, frame.steps[1:], front_step, tail_step)

                rounds(act, body)

            def experts(number):
                S = moe[number]

                def silu(kk, j):
                    act.wait_ge(*S.at("ug_full", 8 * kk + j + 1))
                    act.activation(sg[:, j % 2, :], ps[:, BANK_G + j % 2, :], ACT.Silu).then_inc(S["sg_ready"], 1)

                for c in range(CHUNKS):
                    act.wait_ge(*S.at("cT_full", c + 1))
                    act.activation(cT[:, 512 * c:512 * c + 512], ps[0:E, c, :], ACT.Copy).then_inc(S["cT_ready"], 1)

                def high_part(kk, j):
                    act.wait_ge(*S.at("h_ready", 8 * kk + j + 1))
                    act.activation(heh[:, j % 4, :], he[:, j % 4, :], ACT.Copy).then_inc(S["h_high"], 1)

                silu(0, 0)

                def body(kk, last):
                    for j in range(8):
                        if not (last and j == 7):
                            silu(kk, j + 1)
                        high_part(kk, j)

                with act.Fori(0, E // 2 - 1) as kk:
                    body(kk, False)
                body(E // 2 - 1, True)
                for c in (1, 3):
                    act.wait_ge(*S.at("down_done", CHUNKS * (E - 1) + c + 1))
                    act.activation(y2T[:, 512 * c:512 * c + 512], ps[:, BANK_ACC + c, :], ACT.Copy)\
                        .then_inc(S["y2T_ready1"], 1)

            program(act, attention, experts)

        @block.gpsimd
        def _(pool):
            pool.wait_ge(loaded_first, 16 * LOADS[0])
            pool.wait_ge(prep, 6)

            def attention(L):
                S = L.signals

                def front_step(b, par, misc, use, turn, bank, kind, i):
                    if kind == "rope" and L.ffn and L.blocks[i][0] == "q":
                        pool.wait_ge(*S.at("cos_ready", L.ropes * b + i + 1))
                        pool.wait_ge(*S.at(f"misc_free{bank}", turn + 1))
                        if later(b):
                            pool.wait_ge(*S.at("scores_full", 8 * (b - 1)))
                        pool.tensor_tensor(qT[:, par, block_of(L, i), :], rot_a[:, i % 2, :], rot_b[:, i % 2, :], ALU.add)\
                            .then_inc(S["q_ready"], 1)
                    if kind == "rope" and not L.ffn:
                        pool.wait_ge(*S.at("cos_ready", L.ropes * b + i + 1))
                        pool.wait_ge(*S.at(f"misc_free{bank}", turn + 1))
                        if later(b):
                            pool.wait_ge(*S.at("scores_full", 8 * (b - 1)))
                        if i == 0:
                            pool.tensor_tensor(kT[:, :], rot_a[:, 0, :], rot_b[:, 0, :], ALU.add)\
                                .then_inc(S["kT_ready"], 1)
                        else:
                            pool.tensor_tensor(qT[:, par, 0, :], rot_a[:, 1, :], rot_b[:, 1, :], ALU.add)\
                                .then_inc(S["q_ready"], 1)

                def residual_base(b, par):
                    pool.wait_ge(*S.at("xn_ready", 2 * b + 2))
                    if later(b):
                        pool.wait_ge(*S.at("x1_ready", 2 * b - 2))
                    for t in range(2):
                        last = pool.tensor_tensor(base[:, par, t, :], xn[:, t, :], row[:, R_PB:R_PB + D], ALU.add)
                    last.then_inc(S["base_ready"], 1)

                def spread_keys(b, par, g):
                    pool.wait_ge(*S.at("kT_ready", b + 1))
                    shape = [P, 4, T]
                    pool.tensor_tensor(
                        kz[:, par, 4 * g:4 * g + 4, :], kT[:, :].unsqueeze(1).broadcast_to(shape),
                        head_mask[:, 4 * g:4 * g + 4].unsqueeze(2).broadcast_to(shape), ALU.mult)\
                        .then_inc(S["k_ready"], 1)

                def tail_step(k, misc, use, turn, bank, kind, arg):
                    pass

                def root(b):
                    n = 2 if L.ffn else 1
                    pool.wait_ge(*S.at("pow_ready", n * b + n))
                    if later(b):
                        pool.wait_ge(*S.at("normed", 2 * b))
                    pool.tensor_tensor(rstd[:, 0:n, :], powers[:, 0:n, :],
                                       minus_half[:, 0:2 * n].rearrange("p (n t) -> p n t", n=n), ALU.pow)\
                        .then_inc(S["rstd"], 1)

                def rms_norm(k, lt):
                    tile = 4 * k + lt
                    pool.wait_ge(*S.at("square_ready", tile + 1))
                    pool.tensor_tensor(msq_eps[:, :], msq[:, :], eps[:, :], ALU.add).then_inc(S["rms_step"], 1)
                    pool.wait_ge(*S.at("rms_step", 2 * tile + 1))
                    pool.tensor_tensor(rms[:, :], msq_eps[:, :], minus_half[:, 0:1], ALU.pow)\
                        .then_inc(S["rms_step"], 1)
                    pool.wait_ge(*S.at("rms_step", 2 * tile + 2))
                    pool.tensor_tensor(h2[:, :], x1[:, :], rms[:, 0:1].broadcast_to([P, D]), ALU.mult).then_inc(S["h2_ready"], 1)

                def combine(k, lt):
                    tile = 4 * k + lt
                    step = 5 * tile
                    shape = [P, TOPK, E]
                    pool.wait_ge(*S.at("top_exp", tile + 1))
                    pool.tensor_tensor(rsum[:, :], esum[:, :], minus_one[:, :], ALU.pow)\
                        .then_inc(S["combine_step"], 1)
                    pool.wait_ge(*S.at("combine_step", step + 1))
                    pool.tensor_tensor(wtop[:, :], etop[:, :], rsum[:, 0:1].broadcast_to([P, TOPK]), ALU.mult)\
                        .then_inc(S["combine_step"], 1)
                    pool.wait_ge(*S.at("gate_step", 5 * tile + 5))
                    pool.wait_ge(*S.at("combine_step", step + 2))
                    pool.tensor_tensor(picks[:, :, :], picks[:, :, :], wtop[:, :].unsqueeze(2).broadcast_to(shape),
                                       ALU.mult).then_inc(S["combine_step"], 1)
                    pool.wait_ge(*S.at("combine_step", step + 3))
                    pool.tensor_tensor(pairs[:, :, :], picks[:, 0:2, :], picks[:, 2:4, :], ALU.add)\
                        .then_inc(S["combine_step"], 1)
                    pool.wait_ge(*S.at("combine_step", step + 4))
                    pool.tensor_tensor(comb[:, bass.ds(tile * E, E)], pairs[:, 0, :], pairs[:, 1, :], ALU.add)\
                        .then_inc(S["combine_step"], 1)

                def normalise(k, lt):
                    tile = 4 * k + lt
                    w = L.width
                    shape = [P, H, w]
                    y = yraw[:, lt % 2, 0:H * w].rearrange("p (h w) -> p h w", h=H)
                    pool.wait_ge(*S.at("rinv_ready", tile + 1))
                    pool.wait_ge(*S.at("yraw_ready", UNITS * k + 4 * lt + 4))
                    if not L.ffn:
                        nv = nully[:, :].rearrange("p (h w) -> p h w", h=H)
                        vn = row[:, R_VN:R_VN + P].rearrange("p (h w) -> p h w", h=H)
                        pool.tensor_tensor(nv, vn, sexp[:, lt % 2, :].unsqueeze(2).broadcast_to(shape), ALU.mult)\
                            .then_inc(S["null_step"], 1)
                        pool.wait_ge(*S.at("null_step", 2 * tile + 1))
                        pool.tensor_tensor(y, y, nv, ALU.add).then_inc(S["null_step"], 1)
                        pool.wait_ge(*S.at("null_step", 2 * tile + 2))
                    pool.tensor_tensor(yn[:, 0:H * w].rearrange("p (h w) -> p h w", h=H), y,
                                       rinv[:, lt % 2, :].unsqueeze(2).broadcast_to(shape), ALU.mult)\
                        .then_inc(S["yn_ready"], 1)

                root(0)
                if L.ffn:
                    residual_base(0, 0)
                first_front(L, front_step)
                if not L.ffn:
                    for g in range(G):
                        spread_keys(0, 0, g)

                def body(k, part):
                    for frame in L.plan[part]:
                        for kk, lt in at_slot(frame, k, [4 * lt + 5 + L.lag for lt in range(4)]):
                            normalise(kk, lt)
                        for b, par in ahead_at(frame, k, part, 3):
                            root(b)
                        if L.ffn:
                            for b, par in ahead_at(frame, k, part, 6):
                                residual_base(b, par)
                        take(k, frame.steps, front_step, tail_step)
                        if L.ffn:
                            for kk, lt in at_slot(frame, k, (13, 17, 21, 25)):
                                combine(kk, lt)
                            for kk, lt in at_slot(frame, k, (9, 13, 17, 21)):
                                rms_norm(kk, lt)
                        if not L.ffn:
                            for g in range(G):
                                for b, par in ahead_at(frame, k, part, 5 + g):
                                    spread_keys(b, par, g)

                rounds(pool, body)

            def experts(number):
                S = moe[number]

                def scale(kk, j):
                    e, s, c = kk * 2 + j // 4, j // 4, j % 4
                    if c == 0:
                        pool.wait_ge(*S.at(f"cb_loaded{s}", (kk + 1) * 16))
                    pool.wait_ge(*S.at("hu_ready", 8 * kk + j + 1))
                    pool.tensor_tensor(he[:, j % 4, :], hu[:, j % 4, :], cb[:, s, 512 * c:512 * c + 512], ALU.mult)\
                        .then_inc(S["h_ready"], 1)

                with pool.Fori(0, E // 2) as kk:
                    for j in range(8):
                        scale(kk, j)

            program(pool, attention, experts)


def kernel(**inputs):
    import concourse.bacc as bacc
    from concourse.bass_utils import run_bass_kernel_spmd

    a = {name.replace("L0_", ""): np.asarray(value) for name, value in inputs.items()}

    def partners(w, group, half):
        n = w.shape[-1]
        parts = w.reshape(w.shape[:-1] + (n // group, 2, group // 2)) if half else \
            w.reshape(w.shape[:-1] + (n // 2, 2, 1))
        return parts[..., ::-1, :].reshape(w.shape)

    qkv, bias = a["ffn_qkv_w"], a["ffn_qkv_b"]
    nqk = (QB + KB) * P
    proj = a["ffn_proj_w"].reshape(QB, P, D).transpose(1, 0, 2).reshape(P, QB * D)
    ffn_w = np.concatenate([qkv[:, :nqk], partners(qkv[:, :nqk], 2, False), qkv[:, nqk:], proj, a["ffn_gate_w"]], axis=1)

    def joint(kind, swap):
        geo = a[f"attn_w{kind}_geo"]
        return np.concatenate([a[f"attn_w{kind}_sem"], partners(geo, HD, True) if swap else geo], axis=1)

    mid_w = np.concatenate([joint("q", False), joint("q", True), joint("k", False), joint("k", True),
                            a["attn_wv"], a["attn_wo"]], axis=1)
    null = np.concatenate([a["attn_k_sem_null"], a["attn_k_geo_null"]])[:, None]
    columns = np.concatenate([bias[:nqk].reshape(-1, P).T, partners(bias[:nqk], 2, False).reshape(-1, P).T,
                              a["ffn_attn_norm_w"][:, None], a["ffn_ffn_norm_w"][:, None], null], axis=1)
    rows = np.concatenate([bias[nqk:], a["ffn_proj_b"], a["ffn_attn_sink"], a["ffn_gate_b"], a["attn_v_null"]])[None, :]
    table, masks = shape_constants()
    host = {"x": a["attn_x"], "table": table, "masks": masks, "ffn_w": ffn_w, "mid_w": mid_w, "columns": columns,
            "rows": rows, "w_up": a["ffn_W_up"], "w_down": a["ffn_W_down"]}

    nc = bacc.Bacc("TRN2", target_bir_lowering=False, num_devices=1)
    arrays, args = {}, {}
    for name, value in host.items():
        value = np.ascontiguousarray(value)
        arrays[f"in_{name}"] = value
        args[name] = nc.dram_tensor(f"in_{name}", value.shape, mybir.dt.from_np(value.dtype), kind="ExternalInput").ap()
    out = nc.dram_tensor("out_x", (BATCH, T, D), F32, kind="ExternalOutput").ap()
    build(nc, out=out, **args)
    result = run_bass_kernel_spmd(nc, [arrays], core_ids=[0])
    return result.results[0]["out_x"]
```
